# Optimizing a Trainium2 kernel written in Bass

```python
import numpy as np
import jax
import jax.numpy as jnp

def _softmax(x, axis=-1):
    return jax.nn.softmax(x, axis=axis)

def _gelu(x):
    return jax.nn.gelu(x, approximate=True)

def _silu(x):
    return jax.nn.silu(x)

def _sigmoid(x):
    return jax.nn.sigmoid(x)

def _layernorm(x, axis=-1, eps=1e-05):
    m = jnp.mean(x, axis=axis, keepdims=True)
    v = jnp.var(x, axis=axis, keepdims=True)
    return (x - m) / jnp.sqrt(v + eps)

def _scatter_add(tgt, idx, src, axis=0):
    return tgt.at[idx].add(src)

def _segment_sum(src, seg, n):
    return jax.ops.segment_sum(src, seg, n)
kernel_name = 'mk_xattn_seq_d2_seqx_r4_06a0a1'

def setup_inputs(seed: int=0):
    np.random.seed(seed)
    _w = jnp.asarray

    def _rec_inputs():
        import jax
        import jax.numpy as jnp
        _rk = jax.random.key(seed)
        x = -0.0005207 + 1.001 * jax.random.normal(jax.random.fold_in(_rk, 1), (8, 100, 512), jnp.float32)
        _lenS = 100 - jax.random.randint(jax.random.fold_in(_rk, 7), (8,), 0, max(1, 100 // 4) + 1, jnp.int32)
        _lenS2 = 361 - jax.random.randint(jax.random.fold_in(_rk, 8), (8,), 0, max(1, 361 // 4) + 1, jnp.int32)
        _ctx_2048P = jax.random.normal(jax.random.fold_in(_rk, 11), (8, 16, 512), jnp.float32)
        _ctx_2048c = jax.random.dirichlet(jax.random.fold_in(_rk, 511), 0.3 * jnp.ones((16,), jnp.float32), (8, 361))
        _ctx_2048t = jnp.einsum('bsk,bkd->bsd', _ctx_2048c, _ctx_2048P)
        _ctx_2048t = _ctx_2048t * jax.lax.rsqrt(jnp.mean(jnp.square(_ctx_2048t)) + 1e-12) * 0.953939
        ctx_2048 = 2.81802e-05 + 1.00001 * (_ctx_2048t + 0.3 * jax.random.normal(jax.random.fold_in(_rk, 611), (8, 361, 512), jnp.float32))
        _validS = jnp.arange(100)[None, :] < _lenS[:, None]
        _validS2 = jnp.arange(361)[None, :] < _lenS2[:, None]
        _causal = jnp.tril(jnp.ones((100, 100), dtype=bool))
        mask_BxS2_bf1 = jnp.ones((8, 361), dtype=bool)
        return (x, ctx_2048, mask_BxS2_bf1)
    x, ctx_2048, mask_BxS2_bf1 = _rec_inputs()

    def _L0_xattn_setup():
        import jax, jax.numpy as jnp
        import numpy as np
        B, Q, S1, S2 = (4, 64, 512, 512)
        D, H, K, F = (512, 16, 128, 2048)
        LN_EPS = 1e-05

        def _layer_norm(x, scale, offset):
            mu = jnp.mean(x, axis=-1, keepdims=True)
            var = jnp.var(x, axis=-1, keepdims=True)
            return (x - mu) * jax.lax.rsqrt(var + LN_EPS) * scale + offset

        def _cross_attention(q_in, kv_in, wq, bq, wk, bk, wv, bv, wo, bo, bias_k, bias_v):
            b, q_len, _ = q_in.shape
            t = kv_in.shape[1]
            qh = (q_in @ wq + bq).reshape(b, q_len, H, K)
            kh = (kv_in @ wk + bk).reshape(b, t, H, K)
            vh = (kv_in @ wv + bv).reshape(b, t, H, K)
            kh = jnp.concatenate([kh, jnp.broadcast_to(bias_k, (b, 1, H, K))], axis=1)
            vh = jnp.concatenate([vh, jnp.broadcast_to(bias_v, (b, 1, H, K))], axis=1)
            scale = jnp.sqrt(jnp.asarray(K, q_in.dtype))
            logits = jnp.einsum('bqhk,bthk->bhqt', qh, kh) / scale
            weights = jax.nn.softmax(logits, axis=-1)
            ctx = jnp.einsum('bhqt,bthk->bqhk', weights, vh).reshape(b, q_len, H * K)
            return ctx @ wo + bo

        def _forward(x, xf_1, xf_2, ln1_scale, ln1_offset, wq1, bq1, wk1, bk1, wv1, bv1, wo1, bo1, bias_k1, bias_v1, ln2_scale, ln2_offset, wq2, bq2, wk2, bk2, wv2, bv2, wo2, bo2, bias_k2, bias_v2, ln_mlp_scale, ln_mlp_offset, w_fc1, b_fc1, w_fc2, b_fc2):
            res = x
            h = _layer_norm(x, ln1_scale, ln1_offset)
            x = res + _cross_attention(h, xf_1, wq1, bq1, wk1, bk1, wv1, bv1, wo1, bo1, bias_k1, bias_v1)
            res = x
            h = _layer_norm(x, ln2_scale, ln2_offset)
            x = res + _cross_attention(h, xf_2, wq2, bq2, wk2, bk2, wv2, bv2, wo2, bo2, bias_k2, bias_v2)
            h = _layer_norm(x, ln_mlp_scale, ln_mlp_offset)
            h = jax.nn.gelu(h @ w_fc1 + b_fc1, approximate=False) @ w_fc2 + b_fc2
            return x + h
        key = jax.random.key(seed)
        ks = iter(jax.random.split(key, 64))

        def rn(shape, s=0.02):
            return jax.random.normal(next(ks), shape, jnp.float32) * s
        inp = {'x': rn((B, Q, D), 1.0), 'xf_1': rn((B, S1, D), 1.0), 'xf_2': rn((B, S2, D), 1.0)}
        for i in (1, 2):
            inp[f'ln{i}_scale'] = jnp.ones((D,), jnp.float32)
            inp[f'ln{i}_offset'] = jnp.zeros((D,), jnp.float32)
            inp[f'wq{i}'] = rn((D, H * K))
            inp[f'bq{i}'] = jnp.zeros((H * K,), jnp.float32)
            inp[f'wk{i}'] = rn((D, H * K))
            inp[f'bk{i}'] = jnp.zeros((H * K,), jnp.float32)
            inp[f'wv{i}'] = rn((D, H * K))
            inp[f'bv{i}'] = jnp.zeros((H * K,), jnp.float32)
            inp[f'wo{i}'] = rn((H * K, D))
            inp[f'bo{i}'] = jnp.zeros((D,), jnp.float32)
            inp[f'bias_k{i}'] = rn((1, 1, H, K))
            inp[f'bias_v{i}'] = rn((1, 1, H, K))
        inp['ln_mlp_scale'] = jnp.ones((D,), jnp.float32)
        inp['ln_mlp_offset'] = jnp.zeros((D,), jnp.float32)
        inp['w_fc1'] = rn((D, F))
        inp['b_fc1'] = jnp.zeros((F,), jnp.float32)
        inp['w_fc2'] = rn((F, D))
        inp['b_fc2'] = jnp.zeros((D,), jnp.float32)
        return inp
    _L0_xattn_all = _L0_xattn_setup()
    _L0_xattn_in = {k: v for k, v in _L0_xattn_all.items() if k in ('ln1_scale', 'ln1_offset', 'wq1', 'bq1', 'wk1', 'bk1', 'wv1', 'bv1', 'wo1', 'bo1', 'bias_k1', 'bias_v1', 'ln2_scale', 'ln2_offset', 'wq2', 'bq2', 'wk2', 'bk2', 'wv2', 'bv2', 'wo2', 'bo2', 'bias_k2', 'bias_v2', 'ln_mlp_scale', 'ln_mlp_offset', 'w_fc1', 'b_fc1', 'w_fc2', 'b_fc2')}
    del _L0_xattn_all

    def _L1_xattn_setup():
        import jax, jax.numpy as jnp
        import numpy as np
        D = 512
        H = 16
        HD = D // H
        INNER = 4 * D
        EPS = 1e-05

        def layer_norm(x, w, b):
            mu = jnp.mean(x, axis=-1, keepdims=True)
            var = jnp.mean(jnp.square(x - mu), axis=-1, keepdims=True)
            return (x - mu) * jax.lax.rsqrt(var + EPS) * w + b
        key = jax.random.key(seed)
        ks = jax.random.split(key, 12)
        B, LQ, LK = (4, 256, 512)
        std = 0.02
        inp = {'hidden_states': jax.random.normal(ks[0], (B, LQ, D), jnp.float32), 'encoder_hidden_states': jax.random.normal(ks[1], (B, LK, D), jnp.float32), 'encoder_attention_mask': jnp.ones((B, LK), dtype=bool), 'ln1_w': jnp.ones((D,), jnp.float32), 'ln1_b': jnp.zeros((D,), jnp.float32), 'q_w': jax.random.normal(ks[2], (D, D), jnp.float32) * std, 'q_b': jnp.zeros((D,), jnp.float32), 'k_w': jax.random.normal(ks[3], (D, D), jnp.float32) * std, 'k_b': jnp.zeros((D,), jnp.float32), 'v_w': jax.random.normal(ks[4], (D, D), jnp.float32) * std, 'v_b': jnp.zeros((D,), jnp.float32), 'cproj_w': jax.random.normal(ks[5], (D, D), jnp.float32) * std, 'cproj_b': jnp.zeros((D,), jnp.float32), 'ln2_w': jnp.ones((D,), jnp.float32), 'ln2_b': jnp.zeros((D,), jnp.float32), 'fc_w': jax.random.normal(ks[6], (D, INNER), jnp.float32) * std, 'fc_b': jnp.zeros((INNER,), jnp.float32), 'proj_w': jax.random.normal(ks[7], (INNER, D), jnp.float32) * std, 'proj_b': jnp.zeros((D,), jnp.float32)}
        return inp
    _L1_xattn_all = _L1_xattn_setup()
    _L1_xattn_in = {k: v for k, v in _L1_xattn_all.items() if k in ('ln1_w', 'ln1_b', 'q_w', 'q_b', 'k_w', 'k_b', 'v_w', 'v_b', 'cproj_w', 'cproj_b', 'ln2_w', 'ln2_b', 'fc_w', 'fc_b', 'proj_w', 'proj_b')}
    del _L1_xattn_all
    return {'x': x, 'ctx_2048': ctx_2048, 'mask_BxS2_bf1': mask_BxS2_bf1, 'L0_xattn_ln1_scale': _L0_xattn_in['ln1_scale'], 'L0_xattn_ln1_offset': _L0_xattn_in['ln1_offset'], 'L0_xattn_wq1': _L0_xattn_in['wq1'], 'L0_xattn_bq1': _L0_xattn_in['bq1'], 'L0_xattn_wk1': _L0_xattn_in['wk1'], 'L0_xattn_bk1': _L0_xattn_in['bk1'], 'L0_xattn_wv1': _L0_xattn_in['wv1'], 'L0_xattn_bv1': _L0_xattn_in['bv1'], 'L0_xattn_wo1': _L0_xattn_in['wo1'], 'L0_xattn_bo1': _L0_xattn_in['bo1'], 'L0_xattn_bias_k1': _L0_xattn_in['bias_k1'], 'L0_xattn_bias_v1': _L0_xattn_in['bias_v1'], 'L0_xattn_ln2_scale': _L0_xattn_in['ln2_scale'], 'L0_xattn_ln2_offset': _L0_xattn_in['ln2_offset'], 'L0_xattn_wq2': _L0_xattn_in['wq2'], 'L0_xattn_bq2': _L0_xattn_in['bq2'], 'L0_xattn_wk2': _L0_xattn_in['wk2'], 'L0_xattn_bk2': _L0_xattn_in['bk2'], 'L0_xattn_wv2': _L0_xattn_in['wv2'], 'L0_xattn_bv2': _L0_xattn_in['bv2'], 'L0_xattn_wo2': _L0_xattn_in['wo2'], 'L0_xattn_bo2': _L0_xattn_in['bo2'], 'L0_xattn_bias_k2': _L0_xattn_in['bias_k2'], 'L0_xattn_bias_v2': _L0_xattn_in['bias_v2'], 'L0_xattn_ln_mlp_scale': _L0_xattn_in['ln_mlp_scale'], 'L0_xattn_ln_mlp_offset': _L0_xattn_in['ln_mlp_offset'], 'L0_xattn_w_fc1': _L0_xattn_in['w_fc1'], 'L0_xattn_b_fc1': _L0_xattn_in['b_fc1'], 'L0_xattn_w_fc2': _L0_xattn_in['w_fc2'], 'L0_xattn_b_fc2': _L0_xattn_in['b_fc2'], 'L1_xattn_ln1_w': _L1_xattn_in['ln1_w'], 'L1_xattn_ln1_b': _L1_xattn_in['ln1_b'], 'L1_xattn_q_w': _L1_xattn_in['q_w'], 'L1_xattn_q_b': _L1_xattn_in['q_b'], 'L1_xattn_k_w': _L1_xattn_in['k_w'], 'L1_xattn_k_b': _L1_xattn_in['k_b'], 'L1_xattn_v_w': _L1_xattn_in['v_w'], 'L1_xattn_v_b': _L1_xattn_in['v_b'], 'L1_xattn_cproj_w': _L1_xattn_in['cproj_w'], 'L1_xattn_cproj_b': _L1_xattn_in['cproj_b'], 'L1_xattn_ln2_w': _L1_xattn_in['ln2_w'], 'L1_xattn_ln2_b': _L1_xattn_in['ln2_b'], 'L1_xattn_fc_w': _L1_xattn_in['fc_w'], 'L1_xattn_fc_b': _L1_xattn_in['fc_b'], 'L1_xattn_proj_w': _L1_xattn_in['proj_w'], 'L1_xattn_proj_b': _L1_xattn_in['proj_b']}

def reference(x, ctx_2048, mask_BxS2_bf1, L0_xattn_ln1_scale, L0_xattn_ln1_offset, L0_xattn_wq1, L0_xattn_bq1, L0_xattn_wk1, L0_xattn_bk1, L0_xattn_wv1, L0_xattn_bv1, L0_xattn_wo1, L0_xattn_bo1, L0_xattn_bias_k1, L0_xattn_bias_v1, L0_xattn_ln2_scale, L0_xattn_ln2_offset, L0_xattn_wq2, L0_xattn_bq2, L0_xattn_wk2, L0_xattn_bk2, L0_xattn_wv2, L0_xattn_bv2, L0_xattn_wo2, L0_xattn_bo2, L0_xattn_bias_k2, L0_xattn_bias_v2, L0_xattn_ln_mlp_scale, L0_xattn_ln_mlp_offset, L0_xattn_w_fc1, L0_xattn_b_fc1, L0_xattn_w_fc2, L0_xattn_b_fc2, L1_xattn_ln1_w, L1_xattn_ln1_b, L1_xattn_q_w, L1_xattn_q_b, L1_xattn_k_w, L1_xattn_k_b, L1_xattn_v_w, L1_xattn_v_b, L1_xattn_cproj_w, L1_xattn_cproj_b, L1_xattn_ln2_w, L1_xattn_ln2_b, L1_xattn_fc_w, L1_xattn_fc_b, L1_xattn_proj_w, L1_xattn_proj_b):
    import jax
    import jax.numpy as jnp

    def _L0_xattn_ref(x, xf_1, xf_2, ln1_scale, ln1_offset, wq1, bq1, wk1, bk1, wv1, bv1, wo1, bo1, bias_k1, bias_v1, ln2_scale, ln2_offset, wq2, bq2, wk2, bk2, wv2, bv2, wo2, bo2, bias_k2, bias_v2, ln_mlp_scale, ln_mlp_offset, w_fc1, b_fc1, w_fc2, b_fc2):
        import jax, jax.numpy as jnp
        import numpy as np
        B, Q, S1, S2 = (4, 64, 512, 512)
        D, H, K, F = (512, 16, 128, 2048)
        LN_EPS = 1e-05

        def _layer_norm(x, scale, offset):
            mu = jnp.mean(x, axis=-1, keepdims=True)
            var = jnp.var(x, axis=-1, keepdims=True)
            return (x - mu) * jax.lax.rsqrt(var + LN_EPS) * scale + offset

        def _cross_attention(q_in, kv_in, wq, bq, wk, bk, wv, bv, wo, bo, bias_k, bias_v):
            b, q_len, _ = q_in.shape
            t = kv_in.shape[1]
            qh = (q_in @ wq + bq).reshape(b, q_len, H, K)
            kh = (kv_in @ wk + bk).reshape(b, t, H, K)
            vh = (kv_in @ wv + bv).reshape(b, t, H, K)
            kh = jnp.concatenate([kh, jnp.broadcast_to(bias_k, (b, 1, H, K))], axis=1)
            vh = jnp.concatenate([vh, jnp.broadcast_to(bias_v, (b, 1, H, K))], axis=1)
            scale = jnp.sqrt(jnp.asarray(K, q_in.dtype))
            logits = jnp.einsum('bqhk,bthk->bhqt', qh, kh) / scale
            weights = jax.nn.softmax(logits, axis=-1)
            ctx = jnp.einsum('bhqt,bthk->bqhk', weights, vh).reshape(b, q_len, H * K)
            return ctx @ wo + bo

        def _forward(x, xf_1, xf_2, ln1_scale, ln1_offset, wq1, bq1, wk1, bk1, wv1, bv1, wo1, bo1, bias_k1, bias_v1, ln2_scale, ln2_offset, wq2, bq2, wk2, bk2, wv2, bv2, wo2, bo2, bias_k2, bias_v2, ln_mlp_scale, ln_mlp_offset, w_fc1, b_fc1, w_fc2, b_fc2):
            res = x
            h = _layer_norm(x, ln1_scale, ln1_offset)
            x = res + _cross_attention(h, xf_1, wq1, bq1, wk1, bk1, wv1, bv1, wo1, bo1, bias_k1, bias_v1)
            res = x
            h = _layer_norm(x, ln2_scale, ln2_offset)
            x = res + _cross_attention(h, xf_2, wq2, bq2, wk2, bk2, wv2, bv2, wo2, bo2, bias_k2, bias_v2)
            h = _layer_norm(x, ln_mlp_scale, ln_mlp_offset)
            h = jax.nn.gelu(h @ w_fc1 + b_fc1, approximate=False) @ w_fc2 + b_fc2
            return x + h
        return _forward(x, xf_1, xf_2, ln1_scale, ln1_offset, wq1, bq1, wk1, bk1, wv1, bv1, wo1, bo1, bias_k1, bias_v1, ln2_scale, ln2_offset, wq2, bq2, wk2, bk2, wv2, bv2, wo2, bo2, bias_k2, bias_v2, ln_mlp_scale, ln_mlp_offset, w_fc1, b_fc1, w_fc2, b_fc2)

    def _L1_xattn_ref(hidden_states, encoder_hidden_states, encoder_attention_mask, ln1_w, ln1_b, q_w, q_b, k_w, k_b, v_w, v_b, cproj_w, cproj_b, ln2_w, ln2_b, fc_w, fc_b, proj_w, proj_b):
        import jax, jax.numpy as jnp
        import numpy as np
        D = 512
        H = 16
        HD = D // H
        INNER = 4 * D
        EPS = 1e-05

        def layer_norm(x, w, b):
            mu = jnp.mean(x, axis=-1, keepdims=True)
            var = jnp.mean(jnp.square(x - mu), axis=-1, keepdims=True)
            return (x - mu) * jax.lax.rsqrt(var + EPS) * w + b
        B, LQ, _ = hidden_states.shape
        LK = encoder_hidden_states.shape[1]
        residual = hidden_states
        x = layer_norm(hidden_states, ln1_w, ln1_b)
        q = (x @ q_w + q_b).reshape(B, LQ, H, HD).transpose(0, 2, 1, 3)
        k = (encoder_hidden_states @ k_w + k_b).reshape(B, LK, H, HD).transpose(0, 2, 1, 3)
        v = (encoder_hidden_states @ v_w + v_b).reshape(B, LK, H, HD).transpose(0, 2, 1, 3)
        scale = 1.0 / np.sqrt(HD).astype(np.float32)
        scores = jnp.einsum('bhqd,bhkd->bhqk', q, k) * scale
        mask = encoder_attention_mask[:, None, None, :]
        mask_value = jnp.finfo(scores.dtype).min
        scores = jnp.where(mask, scores, mask_value)
        attn = jax.nn.softmax(scores, axis=-1)
        out = jnp.einsum('bhqk,bhkd->bhqd', attn, v)
        out = out.transpose(0, 2, 1, 3).reshape(B, LQ, D)
        out = out @ cproj_w + cproj_b
        hidden = out + residual
        residual = hidden
        y = layer_norm(hidden, ln2_w, ln2_b)
        y = jax.nn.gelu(y @ fc_w + fc_b, approximate=True)
        y = y @ proj_w + proj_b
        return residual + y
    x = _L0_xattn_ref(x, ctx_2048, ctx_2048, L0_xattn_ln1_scale, L0_xattn_ln1_offset, L0_xattn_wq1, L0_xattn_bq1, L0_xattn_wk1, L0_xattn_bk1, L0_xattn_wv1, L0_xattn_bv1, L0_xattn_wo1, L0_xattn_bo1, L0_xattn_bias_k1, L0_xattn_bias_v1, L0_xattn_ln2_scale, L0_xattn_ln2_offset, L0_xattn_wq2, L0_xattn_bq2, L0_xattn_wk2, L0_xattn_bk2, L0_xattn_wv2, L0_xattn_bv2, L0_xattn_wo2, L0_xattn_bo2, L0_xattn_bias_k2, L0_xattn_bias_v2, L0_xattn_ln_mlp_scale, L0_xattn_ln_mlp_offset, L0_xattn_w_fc1, L0_xattn_b_fc1, L0_xattn_w_fc2, L0_xattn_b_fc2)
    x = _L1_xattn_ref(x, ctx_2048, mask_BxS2_bf1, L1_xattn_ln1_w, L1_xattn_ln1_b, L1_xattn_q_w, L1_xattn_q_b, L1_xattn_k_w, L1_xattn_k_b, L1_xattn_v_w, L1_xattn_v_b, L1_xattn_cproj_w, L1_xattn_cproj_b, L1_xattn_ln2_w, L1_xattn_ln2_b, L1_xattn_fc_w, L1_xattn_fc_b, L1_xattn_proj_w, L1_xattn_proj_b)
    return x

_drawn_inputs = setup_inputs


def setup_inputs(seed=0):
    import zlib

    import numpy as np

    out = dict(_drawn_inputs(seed))
    spreads = {'L0_xattn_ln1_scale': (1.0, 0.6),
     'L0_xattn_ln1_offset': (0.0, 0.8),
     'L0_xattn_bq1': (0.0, 0.8),
     'L0_xattn_bk1': (0.0, 2.0),
     'L0_xattn_bv1': (0.0, 0.1),
     'L0_xattn_bo1': (0.0, 0.1),
     'L0_xattn_ln2_scale': (1.0, 0.6),
     'L0_xattn_ln2_offset': (0.0, 0.8),
     'L0_xattn_bq2': (0.0, 0.8),
     'L0_xattn_bk2': (0.0, 2.0),
     'L0_xattn_bv2': (0.0, 0.1),
     'L0_xattn_bo2': (0.0, 0.1),
     'L0_xattn_ln_mlp_scale': (1.0, 0.2),
     'L0_xattn_ln_mlp_offset': (0.0, 0.351),
     'L0_xattn_b_fc1': (0.0, 0.1),
     'L0_xattn_b_fc2': (0.0, 0.1),
     'L1_xattn_ln1_w': (1.0, 0.6),
     'L1_xattn_ln1_b': (0.0, 0.8),
     'L1_xattn_q_b': (0.0, 0.8),
     'L1_xattn_k_b': (0.0, 2.0),
     'L1_xattn_v_b': (0.0, 0.1),
     'L1_xattn_cproj_b': (0.0, 0.1),
     'L1_xattn_ln2_w': (1.0, 0.2),
     'L1_xattn_ln2_b': (0.0, 0.36),
     'L1_xattn_fc_b': (0.0, 0.1),
     'L1_xattn_proj_b': (0.0, 0.1)}
    factors = {'L0_xattn_wq1': 3.833,
     'L0_xattn_wk1': 3.742,
     'L0_xattn_bias_k1': 64.0,
     'L0_xattn_bias_v1': 64.0,
     'L0_xattn_wq2': 3.958,
     'L0_xattn_wk2': 3.89,
     'L0_xattn_bias_k2': 64.0,
     'L0_xattn_bias_v2': 64.0,
     'L1_xattn_q_w': 8.0,
     'L1_xattn_k_w': 7.976}
    for name, (base, spread) in spreads.items():
        noise = np.random.default_rng([zlib.crc32(name.encode()), seed]).standard_normal(out[name].shape)
        drawn = base * np.exp(spread * noise) if base else spread * noise
        out[name] = jnp.asarray(drawn.astype(out[name].dtype))
    for name, factor in factors.items():
        out[name] = (out[name] * factor).astype(out[name].dtype)
    return out
```

```python
from contextlib import ExitStack

import concourse.bass as bass
from concourse import mybir

ALU = mybir.AluOpType
ACT = mybir.ActivationFunctionType
F32 = mybir.dt.float32
F32R = mybir.dt.float32r
U8 = mybir.dt.uint8

P = 128
BATCH, LQ, LK, D = 8, 100, 361, 512
NB = BATCH // 2
ROWS = NB * LQ
LT = LK + 1
DC = D // P
TC = 3
TK = [P, P, LT - 2 * P]
HEADS0 = 16
INNER = HEADS0 * P
HG = 4
GROUPS = HEADS0 // HG
UNITS = NB * HG
HD1 = 32
RING = 8
STAGE = 4
MLP_F = 8
MLP_STEPS = INNER // P // MLP_F
SCALE0 = float(P) ** -0.5
SCALE1 = float(HD1) ** -0.5
EPS = 1e-5
FMAX = 3.4028234663852886e38

ATT0_TILES = ([("q", h) for h in range(HG)] + [("k", h) for h in range(HG)]
              + [("v", 0), ("v", 1), ("v", 2), ("o", 0), ("v", 3), ("o", 1), ("o", 2), ("o", 3)])
MLP_TILES = [("a", 0)] + [t for f in range(1, MLP_F) for t in (("a", f), ("b", f - 1))] + [("b", MLP_F - 1)]
ATT1_TILES = [(m, j) for m in "qvkc" for j in range(4)]
HALF_TILES = 2 * GROUPS * len(ATT0_TILES) + 2 * MLP_STEPS * len(MLP_TILES) + len(ATT1_TILES)
ATT0_BASE = [0, GROUPS * len(ATT0_TILES)]
MLP_BASE = [2 * GROUPS * len(ATT0_TILES), HALF_TILES - MLP_STEPS * len(MLP_TILES)]
ATT1_BASE = MLP_BASE[1] - len(ATT1_TILES)
assert all(n % RING == 0 for n in (*ATT0_BASE, *MLP_BASE, ATT1_BASE, HALF_TILES))

COLUMNS = [
    [("L0_xattn_bq1", 16), ("L0_xattn_bk1", 16), ("L0_xattn_bv1", 16), ("L0_xattn_bias_k1", 16),
     ("L0_xattn_bias_v1", 16), ("L0_xattn_bo1", 4), ("L0_xattn_ln1_scale", 4), ("L0_xattn_ln1_offset", 4),
     ("L0_xattn_b_fc1", 16), ("L0_xattn_b_fc2", 4), ("L0_xattn_ln_mlp_scale", 4),
     ("L0_xattn_ln_mlp_offset", 4), ("L1_xattn_ln1_w", 4), ("L1_xattn_ln1_b", 4)],
    [("L0_xattn_bq2", 16), ("L0_xattn_bk2", 16), ("L0_xattn_bv2", 16), ("L0_xattn_bias_k2", 16),
     ("L0_xattn_bias_v2", 16), ("L0_xattn_bo2", 4), ("L0_xattn_ln2_scale", 4), ("L0_xattn_ln2_offset", 4),
     ("L1_xattn_fc_b", 16), ("L1_xattn_q_b", 4), ("L1_xattn_k_b", 4), ("L1_xattn_v_b", 4),
     ("L1_xattn_cproj_b", 4), ("L1_xattn_proj_b", 4)],
    [("L1_xattn_ln2_w", 4), ("L1_xattn_ln2_b", 4)],
]


def column_table():
    at = {}
    for t, group in enumerate(COLUMNS):
        n = t * P
        for name, rows in group:
            at[name] = n
            n += rows
        assert n <= (t + 1) * P
    return at


def build(nc, T, out):
    col = column_table()
    ncol_tiles = len(COLUMNS)
    col_dmas = sum(len(g) for g in COLUMNS)

    norms = [("L0_xattn_ln1_scale", "L0_xattn_ln1_offset", "L0_xattn_bo1", ACT.Exp),
             ("L0_xattn_ln2_scale", "L0_xattn_ln2_offset", "L0_xattn_bo2", ACT.Exp),
             ("L0_xattn_ln_mlp_scale", "L0_xattn_ln_mlp_offset", "L0_xattn_b_fc2", ACT.Gelu),
             ("L1_xattn_ln1_w", "L1_xattn_ln1_b", "L1_xattn_cproj_b", ACT.Exp),
             ("L1_xattn_ln2_w", "L1_xattn_ln2_b", "L1_xattn_proj_b", ACT.Gelu_apprx_tanh)]
    NORMS = len(norms)

    NAT, TRA = TC * D, DC * LT
    ctx_dram = nc.dram_tensor("ctx_parts", [BATCH, P, 2, NAT + TRA], F32, kind="Internal").ap()

    with ExitStack() as ctx:
        def sb(name, shape, dt):
            return ctx.enter_context(nc.sbuf_tensor(name, shape, dt))

        def sem(name):
            return ctx.enter_context(nc.semaphore(name))

        big = sb("big", [P, 2 * ROWS * DC], F32)
        scratch = big[:, 0:DC * ROWS]
        xT = big[:, DC * ROWS:].rearrange("p (c n) -> p c n", c=DC)
        raw_ctx = big[:, 0:2 * NAT].rearrange("p (b t d) -> p b t d", b=2, t=TC)
        centred = scratch.rearrange("p (c n) -> p c n", c=DC)
        p0_all = scratch.rearrange("p (b n) -> p b n", b=NB)
        xio = scratch[:, 0:2 * D].rearrange("p (s d) -> p s d", s=2)
        mask01 = scratch[:, 0:2 * LT].rearrange("p (b n) -> p b n", b=2)
        mask_off = scratch[:, 2 * LT:4 * LT].rearrange("p (b n) -> p b n", b=2)
        hT = sb("hT", [P, 2, DC * ROWS], F32R)
        ring = sb("ring", [P, RING, 2, D], F32R)
        stage = sb("stage", [P, STAGE, D], F32)
        qT = sb("qT", [P, 2, HG * ROWS], F32R)
        ctxT = sb("ctxT", [P, 2, 2, TRA], F32R)
        ctxN = sb("ctxN", [P, 2, NAT], F32R)
        kT = sb("kT", [P, 2, 2, LT], F32R)
        PW = TC * P
        prob = sb("prob", [P, 3, PW], F32)
        pT = sb("pT", [P, 2, 2, TC * ROWS], F32R)
        U = sb("U", [P, 2, DC * HG * ROWS], F32R)
        part = sb("part", [P, 2, 2, ROWS], F32R)
        tmp = sb("tmp", [P, 2, ROWS], F32)
        p0_row = sb("p0_row", [1, ROWS], F32)
        mask_u8 = sb("mask_u8", [P, 2, LK], U8)
        cols = sb("cols", [P, ncol_tiles * P], F32)
        extra_k = sb("extra_k", [P, 2, HEADS0, 2], F32R)
        extra_v = sb("extra_v", [P, 2, HEADS0], F32)
        ident = sb("ident", [P, P], F32)
        mean_w = sb("mean_w", [P, P], F32)
        stat = sb("stat", [P, 16], F32)
        nmax, denom, rden, eps, table_load = stat[:, 0:3], stat[:, 3:6], stat[:, 6:9], stat[:, 9:10], stat[:, 10:12]
        q_masked = U
        attnT = qT
        v1 = [ctxN, hT]

        bank = [ctx.enter_context(nc.psum_tensor(f"bank{i}", [P, 512], F32)) for i in range(8)]

        class S:
            pass

        S.cols_in = sem("cols_in")
        S.cols_cleared = sem("cols_cleared")
        S.ident_cleared = sem("ident_cleared")
        S.ident_ready = sem("ident_ready")
        S.cols_mm = sem("cols_mm")
        S.cols_ready = sem("cols_ready")
        S.prob_cleared = sem("prob_cleared")
        S.mean_ready = sem("mean_ready")
        S.extra_a = sem("extra_a")
        S.extra_ready = sem("extra_ready")
        S.raw_cleared = sem("raw_cleared")
        S.c_mm = sem("c_mm")
        S.c_hi = sem("c_hi")
        S.c_lo = sem("c_lo")
        S.w_hi = sem("w_hi")
        S.w_ready = sem("w_ready")
        S.w_done = sem("w_done")
        S.x_mm = sem("x_mm")
        S.x_ready = sem("x_ready")
        S.out_mm = sem("out_mm")
        S.out_copied = sem("out_copied")
        S.ln_hi = sem("ln_hi")
        S.ln_lo = sem("ln_lo")
        S.ln_mm = sem("ln_mm")
        S.ln_var = sem("ln_var")
        S.ln_cent = sem("ln_cent")
        S.ln_sq = sem("ln_sq")
        S.ln_std = sem("ln_std")
        S.ln_rstd = sem("ln_rstd")
        S.ln_y = sem("ln_y")
        S.ln_bias = sem("ln_bias")
        S.q_hi = sem("q_hi")
        S.q_lo = sem("q_lo")
        S.k_mm = sem("k_mm")
        S.k_hi = sem("k_hi")
        S.k_lo = sem("k_lo")
        S.k_col = sem("k_col")
        S.s_mm = sem("s_mm")
        S.nm_ready = sem("nm_ready")
        S.exp_ready = sem("exp_ready")
        S.rden_ready = sem("rden_ready")
        S.p_ready = sem("p_ready")
        S.t_mm = sem("t_mm")
        S.pt_hi = sem("pt_hi")
        S.pt_lo = sem("pt_lo")
        S.u_mm = sem("u_mm")
        S.u_hi = sem("u_hi")
        S.u_lo = sem("u_lo")
        S.v_tmp = sem("v_tmp")
        S.v_hi = sem("v_hi")
        S.v_lo = sem("v_lo")
        S.x_add = sem("x_add")
        S.p0_add = sem("p0_add")
        S.p0_ready = sem("p0_ready")
        S.m_gelu = sem("m_gelu")
        S.m_hi = sem("m_hi")
        S.m_lo = sem("m_lo")
        S.m_add = sem("m_add")
        S.mask_a = sem("mask_a")
        S.mask_ready = sem("mask_ready")
        S.qz_ready = sem("qz_ready")
        S.q1_hi = sem("q1_hi")
        S.q1_lo = sem("q1_lo")
        S.k1_mm = sem("k1_mm")
        S.k1_hi = sem("k1_hi")
        S.k1_lo = sem("k1_lo")
        S.v1_mm = sem("v1_mm")
        S.v1_hi = sem("v1_hi")
        S.v1_lo = sem("v1_lo")
        S.s1_mm = sem("s1_mm")
        S.nm1_ready = sem("nm1_ready")
        S.exp1_ready = sem("exp1_ready")
        S.rden1_ready = sem("rden1_ready")
        S.p1_ready = sem("p1_ready")
        S.t1_mm = sem("t1_mm")
        S.pt1_hi = sem("pt1_hi")
        S.pt1_lo = sem("pt1_lo")
        S.a_mm = sem("a_mm")
        S.a_hi = sem("a_hi")
        S.a_lo = sem("a_lo")
        S.c_add = sem("c_add")
        S.p1_cleared = sem("p1_cleared")
        S.w_in = [sem(f"w_in{k}") for k in range(STAGE)]
        S.raw_in = [sem(f"raw_in{b}") for b in range(2)]
        S.c_out = [sem(f"c_out{b}") for b in range(2)]
        S.ctxT_in = [sem(f"ctxT_in{b}") for b in range(2)]
        S.ctxN_in = [sem(f"ctxN_in{c}") for c in range(DC)]
        S.x_in = [sem(f"x_in{b}") for b in range(2)]
        S.out_saved = [sem(f"out_saved{b}") for b in range(2)]
        S.mask_in = [sem(f"mask_in{b}") for b in range(2)]
        START = 1

        def split_mms(eng, dst, parts_l, parts_r, first, last):
            order = [(0, 0), (0, 1), (1, 0)]
            for n, (a, b) in enumerate(order):
                mm = eng.matmul(dst, parts_l[a], parts_r[b], start=first and n == 0,
                                stop=last and n == len(order) - 1)
            return mm

        def f32(ap):
            return ap.bitcast(F32)

        def by_chunk(natural):
            return natural.rearrange("p (c t k) -> p t c k", c=DC, t=TC)

        def hT_c(part_, c):
            return hT[:, part_, c * ROWS:(c + 1) * ROWS]

        def w_slot(k):
            return [ring[:, k % RING, p_, :] for p_ in range(2)]

        def w_cols(k, c):
            return [w[:, c * P:(c + 1) * P] for w in w_slot(k)]

        def ctxT_c(buf, c, t0=0, t1=LT):
            return [ctxT[:, buf, p_, c * LT + t0:c * LT + t1] for p_ in range(2)]

        def two(t):
            return [t[:, p_] for p_ in range(2)]

        def att0_step(half, layer, g):
            it = half * (2 * GROUPS) + layer * GROUPS + g
            n = half * HALF_TILES + ATT0_BASE[layer] + g * len(ATT0_TILES)
            return it, n

        def mlp_step(half, m, st):
            M = half * (2 * MLP_STEPS) + m * MLP_STEPS + st
            n = half * HALF_TILES + MLP_BASE[m] + st * len(MLP_TILES)
            return M, n

        T0 = {t: k for k, t in enumerate(ATT0_TILES)}
        TM = {t: k for k, t in enumerate(MLP_TILES)}
        T1 = {t: k for k, t in enumerate(ATT1_TILES)}
        G1 = NB * 4
        U1 = NB * HEADS0

        def ready(n, k):
            return n + (STAGE + k + 1)

        def done(n, k):
            return START + n + (RING + k + 1)

        L0 = [{k: T[f"L0_xattn_{k}{n}"] for k in ("wq", "wk", "wv", "wo")} for n in (1, 2)]
        mlp = [(T["L0_xattn_w_fc1"], T["L0_xattn_w_fc2"], "L0_xattn_b_fc1", ACT.Gelu),
               (T["L1_xattn_fc_w"], T["L1_xattn_proj_w"], "L1_xattn_fc_b", ACT.Gelu_apprx_tanh)]
        L1W = {"q": T["L1_xattn_q_w"], "k": T["L1_xattn_k_w"], "v": T["L1_xattn_v_w"], "c": T["L1_xattn_cproj_w"]}

        def column_tile(w, n):
            return w.rearrange("(c p) n -> p c n", p=P)[:, :, bass.ds(n * P, P)]

        def row_tile(w, n):
            return w.rearrange("(r p) n -> p r n", p=P)[:, bass.ds(n, 1), :]

        def x_complete(l, half, c):
            if l == 0:
                return S.x_ready, half * NB + NB
            if l in (1, 2):
                return S.x_add, START + (half * 2 + l) * (GROUPS * DC) - DC + c + 1
            if l == 3:
                return S.m_add, START + (half * 2 + 1) * (MLP_STEPS * DC) - DC + c + 1
            return S.c_add, half * DC + c + 1

        STEPS0 = range(UNITS + 2)
        APPLY = {(b + 1) * HG + 2: [(b, c) for c in range(DC)] for b in range(NB - 2)}
        APPLY[UNITS] = [(NB - 2, 0), (NB - 2, 1)]
        APPLY[UNITS + 1] = [(NB - 2, 2), (NB - 2, 3)] + [(NB - 1, c) for c in range(DC)]

        block = ctx.enter_context(nc.Block())

        @block.sync
        def _(sp):
            for semaphore in (S.c_hi, S.c_lo, *S.c_out, S.x_mm, S.x_add, S.k_mm, S.u_mm, S.v_tmp, S.p0_ready, S.t_mm,
                              S.m_gelu, S.m_add, *S.out_saved, S.out_copied, S.mask_ready, S.nm1_ready, S.pt1_lo,
                              S.a_lo, S.t1_mm):
                sp.sem_inc(semaphore, START)
            sp.wait_ge(S.cols_cleared, 1)
            for t, group in enumerate(COLUMNS):
                n = 0
                for name, rows in group:
                    src = T[name]
                    if len(src.shape) == 4:
                        src = src.rearrange("a b h k -> (a b h) k")
                    else:
                        src = src.rearrange("(r k) -> r k", k=P)
                    sp.dma_start(prob[n:n + rows, 0, t * P:(t + 1) * P], src).then_inc(S.cols_in, 16)
                    n += rows

            sp.wait_ge(S.raw_cleared, 1)
            with sp.Fori(0, BATCH // 2) as i:
                for b in range(2):
                    sp.wait_ge(S.c_hi, START + i * (2 * (1 + DC)))
                    sp.wait_ge(S.c_lo, START + i * (2 * (1 + DC)))
                    sp.wait_ge(S.raw_cleared, 1)
                    src = T["ctx_2048"][bass.ds(i * 2 + b, 1)].rearrange("o t d -> (o t) d")
                    for t in range(TC):
                        lo, hi = max(0, t * P - 1), min(LK, (t + 1) * P - 1)
                        r0 = 1 if t == 0 else 0
                        sp.dma_start(raw_ctx[r0:r0 + hi - lo, b, t, :], src[lo:hi, :]).then_inc(S.raw_in[b], 16)

            def load_tile(n, k, src):
                reached = sp.to_reg(n + k + 1)
                sp.wait_ge(S.cols_ready, 1)
                sp.wait_ge(S.w_ready, reached)
                dst = stage[:, k % STAGE, :]
                if src.shape[1] == DC:
                    dst = dst.rearrange("p (c n) -> p c n", c=DC)
                else:
                    dst = dst.rearrange("p (r n) -> p r n", r=1)
                sp.dma_start(dst, src).then_inc(S.w_in[k % STAGE], 16)

            def load_ctxT(half, b, buf):
                sp.dma_start(f32(ctxT[:, buf]), ctx_dram[bass.ds(half * NB + b, 1), :, :, NAT:NAT + TRA]
                             .rearrange("o p s n -> p (o s) n")).then_inc(S.ctxT_in[buf], 16)

            def load_ctxN(half, b, c):
                sp.dma_start(f32(ctxN[:, :, c * PW:(c + 1) * PW]),
                             ctx_dram[bass.ds(half * NB + b, 1), :, :, c * PW:(c + 1) * PW]
                             .rearrange("o p s n -> p (o s) n")).then_inc(S.ctxN_in[c], 16)

            def attention0(half, layer):
                w = L0[layer]
                with sp.Fori(0, GROUPS) as g:
                    it, n = att0_step(half, layer, g)

                    def load_tiles(ks):
                        for k in ks:
                            m, h = ATT0_TILES[k]
                            src = w["w" + m]
                            load_tile(n, k, row_tile(src, g * HG + h) if m == "o" else column_tile(src, g * HG + h))

                    reached = sp.to_reg(START + it * ((NB - 1) * HG))
                    sp.wait_ge(S.cols_ready, 1)
                    sp.wait_ge(S.k_mm, reached)
                    load_ctxT(half, 0, 0)
                    reached = sp.to_reg(START + n)
                    sp.wait_ge(S.cols_ready, 1)
                    sp.wait_ge(S.w_done, reached)
                    load_ctxT(half, 1, 1)
                    load_tiles(range(0, RING))
                    reached = sp.to_reg(START + it * (NB * DC))
                    sp.wait_ge(S.cols_ready, 1)
                    sp.wait_ge(S.u_mm, reached)
                    for c in range(DC):
                        load_ctxN(half, 0, c)
                    load_tiles(range(RING, len(ATT0_TILES)))
                    for b in range(1, NB):
                        if b + 1 < NB:
                            reached = sp.to_reg(START + it * ((NB - 1) * HG) + b * HG)
                            sp.wait_ge(S.cols_ready, 1)
                            sp.wait_ge(S.k_mm, reached)
                            load_ctxT(half, b + 1, (b + 1) % 2)
                        for c in range(DC):
                            reached = sp.to_reg(START + it * (NB * DC) + (b - 1) * DC + c + 1)
                            sp.wait_ge(S.cols_ready, 1)
                            sp.wait_ge(S.u_mm, reached)
                            load_ctxN(half, b, c)

            def mlp_loads(half, m):
                wa, wb = mlp[m][:2]
                with sp.Fori(0, MLP_STEPS) as st:
                    _, n = mlp_step(half, m, st)
                    for k, (kind, f) in enumerate(MLP_TILES):
                        load_tile(n, k, (column_tile(wa, st * MLP_F + f) if kind == "a"
                                         else row_tile(wb, st * MLP_F + f)))

            sp.wait_ge(S.c_out[0], START + 32 * (BATCH // 2))
            sp.wait_ge(S.c_out[1], START + 32 * (BATCH // 2))
            with sp.Fori(0, 2) as half:
                for b in range(NB):
                    if b < 2:
                        reached = sp.to_reg(START + half * 32)
                        sp.wait_ge(S.cols_ready, 1)
                        sp.wait_ge(S.out_saved[b], reached)
                    else:
                        reached = sp.to_reg(START + half * NB + b - 1)
                        sp.wait_ge(S.cols_ready, 1)
                        sp.wait_ge(S.x_mm, reached)
                    sp.dma_start(xio[0:LQ, b % 2, :], T["x"][bass.ds(half * NB + b, 1)]
                                 .rearrange("o q d -> (o q) d")).then_inc(S.x_in[b % 2], 16)
                attention0(half, 0)
                attention0(half, 1)
                mlp_loads(half, 0)

                n = half * HALF_TILES + ATT1_BASE

                def load_mask(b):
                    sp.dma_start(mask_u8[0:LQ, b % 2, :], T["mask_BxS2_bf1"][bass.ds(half * NB + b, 1), :]
                                 .broadcast_to([LQ, LK])).then_inc(S.mask_in[b % 2], 16)

                reached = sp.to_reg(done(half * HALF_TILES + (ATT0_BASE[1] + (GROUPS - 1) * len(ATT0_TILES)), RING - 1))
                sp.wait_ge(S.cols_ready, 1)
                sp.wait_ge(S.w_done, reached)
                load_ctxT(half, 0, 0)
                load_ctxT(half, 1, 1)
                reached = sp.to_reg(START + half * NB)
                sp.wait_ge(S.cols_ready, 1)
                sp.wait_ge(S.mask_ready, reached)
                load_mask(0)
                load_mask(1)
                for k, (m, j) in enumerate(ATT1_TILES):
                    if m == "c" and j == 0:
                        for b in range(2, NB):
                            reached = sp.to_reg(START + half * NB + b - 1)
                            sp.wait_ge(S.cols_ready, 1)
                            sp.wait_ge(S.mask_ready, reached)
                            load_mask(b)
                            reached = sp.to_reg(half * ((NB - 1) * 4) + (b - 1) * 4)
                            sp.wait_ge(S.cols_ready, 1)
                            sp.wait_ge(S.k1_mm, reached)
                            load_ctxT(half, b, b % 2)
                    load_tile(n, k, column_tile(L1W[m], j) if m in "qk" else row_tile(L1W[m], j))
                mlp_loads(half, 1)
                for b in range(NB):
                    reached = sp.to_reg(START + half * NB + b + 1)
                    sp.wait_ge(S.cols_ready, 1)
                    sp.wait_ge(S.out_copied, reached)
                    sp.dma_start(out[bass.ds(half * NB + b, 1)].rearrange("o q d -> (o q) d"),
                                 xio[0:LQ, b % 2, :]).then_inc(S.out_saved[b % 2], 16)
            sp.wait_ge(S.out_saved[0], START + 64)
            sp.wait_ge(S.out_saved[1], START + 64)

        @block.gpsimd
        def _(pool):
            pool.sem_inc(S.w_ready, STAGE)
            nc.gpsimd.memset(prob[:], 0.0).then_inc(S.cols_cleared, 1)
            nc.gpsimd.memset(ident[:], 0.0).then_inc(S.ident_cleared, 1)
            pool.wait_ge(S.ident_cleared, 1)
            nc.gpsimd.affine_select(out=ident[:], in_=ident[:], compare_op=ALU.not_equal, fill=1.0, base=0,
                                    pattern=[[-1, P]], channel_multiplier=1).then_inc(S.ident_ready, 1)

            def split_tile(n, k):
                src, (hi, lo) = stage[:, k % STAGE, :], w_slot(k)
                pool.wait_ge(S.w_in[k % STAGE], n * 4 + ((k // STAGE) * 16 + 16))
                reached = pool.to_reg(START + n + k + 1)
                pool.wait_ge(S.cols_ready, 1)
                pool.wait_ge(S.w_done, reached)
                nc.gpsimd.tensor_scalar(hi, src, 1.0, 1.0, ALU.mult, ALU.mult).then_inc(S.w_hi, 1)
                pool.wait_ge(S.w_hi, n + k + 1)
                nc.gpsimd.tensor_tensor(lo, src, f32(hi), ALU.subtract).then_inc(S.w_ready, 1)

            def spread_p0(it, b):
                row0 = [f32(pT[0:1, b % 2, p_, 0:ROWS]) for p_ in range(2)]
                pool.wait_ge(S.pt_hi, it * UNITS + (b + 1) * HG)
                pool.wait_ge(S.pt_lo, it * UNITS + (b + 1) * HG)
                pool.wait_ge(S.p0_ready, START + it * NB + b)
                nc.gpsimd.tensor_tensor(p0_row[:], row0[0], row0[1], ALU.add).then_inc(S.p0_add, 1)
                reached = pool.to_reg(it * NB + b + 1)
                pool.wait_ge(S.cols_ready, 1)
                pool.wait_ge(S.p0_add, reached)
                pool.wait_ge(S.v_tmp, START + it * HG)
                nc.gpsimd.partition_broadcast(p0_all[:, b, :], p0_row[:], P).then_inc(S.p0_ready, 1)

            def attention0(half, layer):
                with pool.Fori(0, GROUPS) as g:
                    it, n = att0_step(half, layer, g)
                    for k in range(12):
                        split_tile(n, k)
                    for b in range(NB - 1):
                        spread_p0(it, b)
                    for k in range(12, 16):
                        split_tile(n, k)
                    spread_p0(it, NB - 1)

            def mlp_tiles(half, m):
                with pool.Fori(0, MLP_STEPS) as st:
                    _, n = mlp_step(half, m, st)
                    for k in range(len(MLP_TILES)):
                        split_tile(n, k)

            with pool.Fori(0, 2) as half:
                attention0(half, 0)
                attention0(half, 1)
                mlp_tiles(half, 0)
                reached = pool.to_reg(START + (half + 1) * (2 * GROUPS * DC))
                pool.wait_ge(S.cols_ready, 1)
                pool.wait_ge(S.x_add, reached)
                for p_ in range(2):
                    nc.gpsimd.memset(f32(q_masked[:, p_, :]), 0.0).then_inc(S.qz_ready, 1)
                n = half * HALF_TILES + ATT1_BASE
                for k in range(8):
                    split_tile(n, k)
                pool.wait_ge(S.ln_hi, (half * NORMS + 4) * DC)
                pool.wait_ge(S.ln_lo, (half * NORMS + 4) * DC)

                def convert_mask(b):
                    if b >= 2:
                        reached = pool.to_reg(START + half * U1 + (b - 1) * HEADS0)
                        pool.wait_ge(S.cols_ready, 1)
                        pool.wait_ge(S.nm1_ready, reached)
                    reached = pool.to_reg(half * 32 + (b // 2 + 1) * 16)
                    pool.wait_ge(S.cols_ready, 1)
                    pool.wait_ge(S.mask_in[b % 2], reached)
                    nc.gpsimd.tensor_scalar(mask01[0:LQ, b % 2, 1:LT], mask_u8[0:LQ, b % 2, :], 1.0, 1.0,
                                            ALU.mult, ALU.mult).then_inc(S.mask_a, 1)
                    reached = pool.to_reg(half * NB + b + 1)
                    pool.wait_ge(S.cols_ready, 1)
                    pool.wait_ge(S.mask_a, reached)
                    nc.gpsimd.tensor_scalar(mask_off[0:LQ, b % 2, 1:LT], mask01[0:LQ, b % 2, 1:LT], -1.0, FMAX,
                                            ALU.add, ALU.mult).then_inc(S.mask_ready, 1)

                convert_mask(0)
                convert_mask(1)
                for k in range(8, 12):
                    split_tile(n, k)
                convert_mask(2)
                convert_mask(3)
                for k in range(12, 16):
                    split_tile(n, k)
                mlp_tiles(half, 1)

        @block.tensor
        def _(pe):
            pe.sem_inc(S.w_done, START + RING)
            pe.wait_ge(S.ident_ready, 1)
            pe.wait_ge(S.cols_in, 16 * col_dmas)
            for t in range(ncol_tiles):
                pe.transpose(bank[0][:, t * P:(t + 1) * P], prob[:, 0, t * P:(t + 1) * P], ident[:])\
                  .then_inc(S.cols_mm, 1)
            pe.wait_ge(S.cols_ready, 1)

            with pe.Fori(0, BATCH // 2) as i:
                for b in range(2):
                    pe.wait_ge(S.raw_in[b], i * (16 * TC) + 16 * TC)
                    pe.wait_ge(S.c_hi, START + i * (2 * (1 + DC)))
                    pe.wait_ge(S.c_lo, START + i * (2 * (1 + DC)))
                    for c in range(DC):
                        for t in range(TC):
                            mm = pe.transpose(bank[b * DC + c][:, t * P:t * P + TK[t]],
                                              raw_ctx[0:TK[t], b, t, c * P:(c + 1) * P],
                                              ident[0:TK[t], 0:TK[t]])
                        mm.then_inc(S.c_mm, 1)
            pe.wait_ge(S.c_hi, START + BATCH * (1 + DC))
            pe.wait_ge(S.c_lo, START + BATCH * (1 + DC))
            pe.wait_ge(S.mean_ready, 1)

            def x_in(half):
                pe.wait_ge(S.out_copied, START + half * NB)
                for b in range(NB):
                    pe.wait_ge(S.x_in[b % 2], half * 32 + (b // 2 + 1) * 16)
                    if b >= 2:
                        pe.wait_ge(S.x_ready, half * NB + b - 1)
                    for c in range(DC):
                        mm = pe.transpose(bank[6 + b % 2][:, c * LQ:(c + 1) * LQ],
                                          xio[0:LQ, b % 2, c * P:(c + 1) * P], ident[0:LQ, 0:LQ])
                    mm.then_inc(S.x_mm, 1)

            def x_out(half):
                pe.wait_ge(S.m_add, START + (half + 1) * (2 * MLP_STEPS * DC))
                for b in range(NB):
                    if b >= 2:
                        pe.wait_ge(S.out_copied, START + half * NB + b - 1)
                    for c in range(DC):
                        mm = pe.transpose(bank[6 + b % 2][0:LQ, c * P:(c + 1) * P],
                                          xT[:, c, b * LQ:(b + 1) * LQ], ident[:])
                    mm.then_inc(S.out_mm, 1)

            def layer_norm(half, l):
                li = half * NORMS + l
                for c in range(DC):
                    pe.wait_ge(*x_complete(l, half, c))
                    mm = pe.matmul(bank[0][:, 0:ROWS], mean_w[:], xT[:, c, :], start=c == 0, stop=c == DC - 1)
                mm.then_inc(S.ln_mm, 1)
                for c in range(DC):
                    pe.wait_ge(S.ln_sq, li * DC + c + 1)
                    pe.matmul(bank[1][:, 0:ROWS], mean_w[:], tmp[:, c % 2, :], start=c == 0, stop=c == DC - 1)\
                      .then_inc(S.ln_var, 1)

            def norm_ready(half, l, c):
                pe.wait_ge(S.ln_hi, (half * NORMS + l) * DC + c + 1)
                pe.wait_ge(S.ln_lo, (half * NORMS + l) * DC + c + 1)

            def attention0(half, layer):
                with pe.Fori(0, GROUPS) as g:
                    it, n = att0_step(half, layer, g)
                    B = it * UNITS
                    for h in range(HG):
                        pe.wait_ge(S.w_ready, ready(n, T0["q", h]))
                        if h >= 2:
                            pe.wait_ge(S.q_lo, it * HG + h - 1)
                        for c in range(DC):
                            if h == 0:
                                norm_ready(half, layer, c)
                            mm = split_mms(pe, bank[h % 2][:, 0:ROWS], w_cols(T0["q", h], c),
                                           [hT_c(0, c), hT_c(1, c)], c == 0, c == DC - 1)
                        mm.then_inc(S.w_done, 1)

                    def keys(u):
                        b, h = divmod(u, HG)
                        if b == 0:
                            pe.wait_ge(S.w_ready, ready(n, T0["k", h]))
                        if h == 0:
                            pe.wait_ge(S.ctxT_in[b % 2], half * (18 * 16) + (layer * 8 + b // 2 + 1) * 16 + g * 32)
                        if u < 2:
                            pe.wait_ge(S.q_lo, it * HG + 3 + u)
                        else:
                            pe.wait_ge(S.k_lo, B + u - 1)
                        for c in range(DC):
                            mm = split_mms(pe, bank[u % 2][:, 0:LT], w_cols(T0["k", h], c),
                                           ctxT_c(b % 2, c), c == 0, c == DC - 1)
                        mm.then_inc(S.w_done if b == NB - 1 else S.k_mm, 1)

                    def logits(u):
                        b, h = divmod(u, HG)
                        pe.wait_ge(S.k_hi, B + u + 1)
                        pe.wait_ge(S.k_lo, B + u + 1)
                        pe.wait_ge(S.k_col, B + u + 1)
                        if u == 0:
                            pe.wait_ge(S.q_hi, it * HG + HG)
                            pe.wait_ge(S.x_add, START + it * DC)
                        if u >= 2:
                            pe.wait_ge(S.nm_ready, B + u - 1)
                        a = h * ROWS + b * LQ
                        split_mms(pe, bank[2 + u % 2][0:LQ, 0:LT], [qT[:, p_, a:a + LQ] for p_ in range(2)],
                                  [kT[:, u % 2, p_, :] for p_ in range(2)], True, True).then_inc(S.s_mm, 1)

                    def transpose_p(u):
                        pe.wait_ge(S.p_ready, B + u + 1)
                        if u >= 2:
                            pe.wait_ge(S.pt_lo, B + u - 1)
                        for t in range(TC):
                            mm = pe.transpose(bank[4 + u % 2][:, t * LQ:(t + 1) * LQ],
                                              prob[0:LQ, u % 3, t * P:(t + 1) * P], ident[0:LQ, 0:LQ])
                        mm.then_inc(S.t_mm, 1)

                    def apply_p(b, c):
                        if c == 0:
                            pe.wait_ge(S.pt_hi, B + (b + 1) * HG)
                            pe.wait_ge(S.pt_lo, B + (b + 1) * HG)
                        pe.wait_ge(S.ctxN_in[c], half * (32 * 16) + (layer * 16 + b + 1) * 16 + g * (NB * 16))
                        m = b * DC + c
                        if m < 2:
                            pe.wait_ge(S.v_tmp, START + it * HG)
                        else:
                            pe.wait_ge(S.u_lo, it * (NB * DC) + m - 1)
                        for t in range(TC):
                            K = TK[t]
                            mm = split_mms(pe, bank[6 + c % 2][:, 0:ROWS],
                                           [ctxN[0:K, p_, (c * TC + t) * P:(c * TC + t + 1) * P] for p_ in range(2)],
                                           [pT[0:K, b % 2, p_, t * ROWS:(t + 1) * ROWS] for p_ in range(2)],
                                           t == 0, t == TC - 1)
                        mm.then_inc(S.u_mm, 1)

                    def values(h):
                        pe.wait_ge(S.w_ready, ready(n, T0["v", h]))
                        if h >= 2:
                            pe.wait_ge(S.v_tmp, START + it * HG + h - 1)
                        for c in range(DC):
                            if h == 0 and c in (0, DC - 1):
                                chunks = (NB - 1) * DC + (DC - 1 if c == 0 else DC)
                                pe.wait_ge(S.u_hi, it * (NB * DC) + chunks)
                                pe.wait_ge(S.u_lo, it * (NB * DC) + chunks)
                            a = (c * HG + h) * ROWS
                            mm = split_mms(pe, bank[6 + h % 2][:, 0:ROWS], w_cols(T0["v", h], c),
                                           [U[:, p_, a:a + ROWS] for p_ in range(2)], c == 0, c == DC - 1)
                        mm.then_inc(S.w_done, 1)

                    def project(h):
                        pe.wait_ge(S.w_ready, ready(n, T0["o", h]))
                        pe.wait_ge(S.v_hi, it * HG + h + 1)
                        pe.wait_ge(S.v_lo, it * HG + h + 1)
                        w = w_slot(T0["o", h])
                        for c in range(DC):
                            mm = split_mms(pe, bank[2 + c][:, 0:ROWS], [x[:, c * P:(c + 1) * P] for x in w],
                                           [part[:, h % 2, p_, :] for p_ in range(2)], h == 0, h == HG - 1)
                        mm.then_inc(S.w_done, 1)

                    for s in STEPS0:
                        if s < UNITS:
                            keys(s)
                        if 1 <= s <= UNITS:
                            logits(s - 1)
                        if s >= 2:
                            transpose_p(s - 2)
                        for b, c in APPLY.get(s, []):
                            apply_p(b, c)
                    for k in range(RING, len(ATT0_TILES)):
                        m, h = ATT0_TILES[k]
                        (values if m == "v" else project)(h)

            def mlp_block(half, m):
                with pe.Fori(0, MLP_STEPS) as st:
                    M, n = mlp_step(half, m, st)

                    def up(f):
                        pe.wait_ge(S.m_gelu, START + M * MLP_F + max(f - 1, 0))
                        for c in range(DC):
                            if f == 0:
                                norm_ready(half, 2 * m + 2, c)
                            mm = split_mms(pe, bank[f % 2][:, 0:ROWS], w_cols(TM["a", f], c),
                                           [hT_c(0, c), hT_c(1, c)], c == 0, c == DC - 1)
                        return mm

                    def down(f):
                        pe.wait_ge(S.m_hi, M * MLP_F + f + 1)
                        pe.wait_ge(S.m_lo, M * MLP_F + f + 1)
                        if f == 0:
                            pe.wait_ge(S.m_add, START + M * DC)
                        w = w_slot(TM["b", f])
                        for c in range(DC):
                            mm = split_mms(pe, bank[2 + c][:, 0:ROWS], [x[:, c * P:(c + 1) * P] for x in w],
                                           [part[:, f % 2, p_, :] for p_ in range(2)], f == 0, f == MLP_F - 1)
                        return mm

                    for k, (kind, f) in enumerate(MLP_TILES):
                        pe.wait_ge(S.w_ready, ready(n, k))
                        (up if kind == "a" else down)(f).then_inc(S.w_done, 1)

            def attention1(half):
                n = half * HALF_TILES + ATT1_BASE
                for j in range(4):
                    pe.wait_ge(S.w_ready, ready(n, T1["q", j]))
                    if j >= 2:
                        pe.wait_ge(S.q1_lo, half * 16 + (j - 1) * HG)
                    for c in range(DC):
                        if j == 0:
                            norm_ready(half, 3, c)
                        mm = split_mms(pe, bank[j % 2][:, 0:ROWS], w_cols(T1["q", j], c),
                                       [hT_c(0, c), hT_c(1, c)], c == 0, c == DC - 1)
                    mm.then_inc(S.w_done, 1)

                def values(b):
                    if b == 0:
                        for j in range(4):
                            pe.wait_ge(S.w_ready, ready(n, T1["v", j]))
                    pe.wait_ge(S.ctxT_in[b % 2], half * (18 * 16) + (17 + b // 2) * 16)
                    if b:
                        pe.wait_ge(S.a_lo, START + half * (G1 * HG) + (4 * b - 2) * HG)
                    for t in range(TC):
                        if t == 2:
                            pe.wait_ge(S.v1_lo, half * (NB * TC) + b * TC + 1)
                        last_use = b == NB - 1 and t == TC - 1
                        for c in range(DC):
                            mm = split_mms(pe, bank[6 + t % 2][0:TK[t], :], ctxT_c(b % 2, c, t * P, t * P + TK[t]),
                                           w_slot(T1["v", c]), c == 0, c == DC - 1)
                            if last_use:
                                mm.then_inc(S.w_done, 1)
                        if not last_use:
                            mm.then_inc(S.v1_mm, 1)

                def keys(s):
                    b, j = divmod(s, 4)
                    if b == 0:
                        pe.wait_ge(S.w_ready, ready(n, T1["k", j]))
                    if s < 2:
                        pe.wait_ge(S.q1_lo, half * 16 + 16)
                    else:
                        pe.wait_ge(S.k1_lo, half * G1 + s - 1)
                    for c in range(DC):
                        mm = split_mms(pe, bank[s % 2][:, 0:LT], w_cols(T1["k", j], c), ctxT_c(b % 2, c),
                                       c == 0, c == DC - 1)
                    mm.then_inc(S.w_done if b == NB - 1 else S.k1_mm, 1)

                def logits(u):
                    s, i = divmod(u, HG)
                    b, j = divmod(s, 4)
                    pe.wait_ge(S.k1_hi, half * G1 + s + 1)
                    pe.wait_ge(S.k1_lo, half * G1 + s + 1)
                    pe.wait_ge(S.nm1_ready, START + half * U1 + max(u - 1, 0))
                    a = (j * HG + i) * ROWS + b * LQ
                    split_mms(pe, bank[2 + u % 2][0:LQ, 0:LT], [q_masked[:, p_, a:a + LQ] for p_ in range(2)],
                              [kT[:, s % 2, p_, :] for p_ in range(2)], True, True).then_inc(S.s1_mm, 1)

                def transpose_p(u):
                    pe.wait_ge(S.p1_ready, half * U1 + u + 1)
                    pe.wait_ge(S.pt1_lo, START + half * U1 + max(u - 1, 0))
                    for t in range(TC):
                        mm = pe.transpose(bank[4 + u % 2][:, t * LQ:(t + 1) * LQ],
                                          prob[0:LQ, u % 3, t * P:(t + 1) * P], ident[0:LQ, 0:LQ])
                    mm.then_inc(S.t1_mm, 1)

                def apply_p(s):
                    b, j = divmod(s, 4)
                    vb = v1[b % 2]
                    pe.wait_ge(S.pt1_hi, half * U1 + (s + 1) * HG)
                    pe.wait_ge(S.pt1_lo, START + half * U1 + (s + 1) * HG)
                    seen = min((s + 2) // 4 + 1, NB) * TC
                    pe.wait_ge(S.v1_hi, half * (NB * TC) + seen)
                    pe.wait_ge(S.v1_lo, half * (NB * TC) + seen)
                    pe.wait_ge(S.a_lo, START + half * (G1 * HG) + max(s - 1, 0) * HG)
                    for t in range(TC):
                        K = TK[t]
                        mm = split_mms(pe, bank[6 + s % 2][:, 0:ROWS],
                                       [vb[0:K, p_, t * D + j * P:t * D + (j + 1) * P] for p_ in range(2)],
                                       [pT[0:K, s % 2, p_, t * ROWS:(t + 1) * ROWS] for p_ in range(2)],
                                       t == 0, t == TC - 1)
                    mm.then_inc(S.a_mm, 1)

                for s in range(G1 + 2):
                    if s < G1:
                        if s % 4 == 0:
                            values(s // 4)
                        keys(s)
                    for i in range(HG):
                        u = (s - 1) * HG + i
                        if 0 <= u < U1:
                            logits(u)
                        if 0 <= u - 2 < U1:
                            transpose_p(u - 2)
                    if s >= 2:
                        apply_p(s - 2)
                pe.wait_ge(S.a_hi, (half + 1) * (G1 * HG))
                pe.wait_ge(S.a_lo, START + (half + 1) * (G1 * HG))
                for j in range(4):
                    pe.wait_ge(S.w_ready, ready(n, T1["c", j]))
                    w = w_slot(T1["c", j])
                    for c in range(DC):
                        mm = split_mms(pe, bank[2 + c][:, 0:ROWS], [x[:, c * P:(c + 1) * P] for x in w],
                                       [attnT[:, p_, j * ROWS:(j + 1) * ROWS] for p_ in range(2)], j == 0, j == 3)
                    mm.then_inc(S.w_done, 1)

            with pe.Fori(0, 2) as half:
                x_in(half)
                layer_norm(half, 0)
                attention0(half, 0)
                layer_norm(half, 1)
                attention0(half, 1)
                layer_norm(half, 2)
                mlp_block(half, 0)
                layer_norm(half, 3)
                pe.wait_ge(S.qz_ready, (half + 1) * 2)
                attention1(half)
                layer_norm(half, 4)
                mlp_block(half, 1)
                x_out(half)

        @block.scalar
        def _(act):
            def high(dst, src, bias=0.0):
                return nc.scalar.activation(dst, src, ACT.Identity, bias=bias)

            act.wait_ge(S.cols_ready, 1)
            with act.Fori(0, BATCH // 2) as i:
                for b in range(2):
                    o = b * (U.shape[2] // 2)
                    act.wait_ge(S.raw_in[b], i * (16 * TC) + 16 * TC)
                    act.wait_ge(S.c_out[b], START + i * 32)
                    high(by_chunk(U[:, 0, o:o + NAT]), raw_ctx[:, b].rearrange("p t (c k) -> p t c k", c=DC))\
                        .then_inc(S.c_hi, 1)
                    for c in range(DC):
                        act.wait_ge(S.c_mm, i * (2 * DC) + b * DC + c + 1)
                        a = o + NAT + c * LT
                        high(U[:, 0, a:a + LT], bank[b * DC + c][:, 0:LT]).then_inc(S.c_hi, 1)
                    act.wait_ge(S.c_hi, START + i * (2 * (1 + DC)) + (b + 1) * (1 + DC))
                    act.wait_ge(S.c_lo, START + i * (2 * (1 + DC)) + (b + 1) * (1 + DC))
                    for p_ in range(2):
                        act.dma_start(ctx_dram[bass.ds(i * 2 + b, 1), :, p_].rearrange("o p n -> p (o n)"),
                                      f32(U[:, p_, o:o + NAT + TRA])).then_inc(S.c_out[b], 16)

            def layer_norm(half, l):
                li = half * NORMS + l
                offset, then = norms[l][1], norms[l][3]
                nc.scalar.activation(table_load[:, 0:1], eps, ACT.Sqrt)
                for c in range(DC):
                    act.wait_ge(S.ln_cent, li * DC + c + 1)
                    if c >= 2:
                        act.wait_ge(S.ln_var, li * DC + c - 1)
                    nc.scalar.activation(tmp[:, c % 2, :], centred[:, c, :], ACT.Square).then_inc(S.ln_sq, 1)
                act.wait_ge(S.ln_var, (li + 1) * DC)
                nc.scalar.activation(tmp[:, 0, :], bank[1][:, 0:ROWS], ACT.Sqrt, bias=eps).then_inc(S.ln_std, 1)
                nc.scalar.activation(table_load[:, 1:2], eps, then)
                for c in range(DC):
                    act.wait_ge(S.ln_y, li * DC + c + 1)
                    high(hT_c(0, c), centred[:, c, :], cols[:, col[offset] + c:col[offset] + c + 1])\
                        .then_inc(S.ln_hi, 1)

            def attention0(half, layer):
                with act.Fori(0, GROUPS) as g:
                    it, n = att0_step(half, layer, g)
                    B = it * UNITS

                    def head_col(name, h):
                        return cols[:, bass.ds(g * HG + (col[f"L0_xattn_{name}{layer + 1}"] + h), 1)]

                    for h in range(HG):
                        reached = act.to_reg(done(n, T0["q", h]))
                        act.wait_ge(S.cols_ready, 1)
                        act.wait_ge(S.w_done, reached)
                        high(qT[:, 0, h * ROWS:(h + 1) * ROWS], bank[h % 2][:, 0:ROWS], head_col("bq", h))\
                            .then_inc(S.q_hi, 1)

                    def keys(u):
                        b, h = divmod(u, HG)
                        if b == NB - 1:
                            reached = act.to_reg(done(n, T0["k", h]))
                            act.wait_ge(S.cols_ready, 1)
                            act.wait_ge(S.w_done, reached)
                        else:
                            reached = act.to_reg(START + it * ((NB - 1) * HG) + u + 1)
                            act.wait_ge(S.cols_ready, 1)
                            act.wait_ge(S.k_mm, reached)
                        high(kT[:, u % 2, 0, 1:LT], bank[u % 2][:, 1:LT], head_col("bk", h)).then_inc(S.k_hi, 1)

                    def p_turned(u):
                        b, h = divmod(u, HG)
                        act.wait_ge(S.t_mm, START + B + u + 1)
                        if h == 0:
                            act.wait_ge(S.p0_ready, START + it * NB + max(b - 1, 0))
                        dst = pT[:, b % 2, 0, :].rearrange("p (t n) -> p t n", t=TC)[:, :, h * LQ:(h + 1) * LQ]
                        high(dst, bank[4 + u % 2][:, 0:TC * LQ].rearrange("p (t n) -> p t n", t=TC))\
                            .then_inc(S.pt_hi, 1)

                    def exponent(u):
                        act.wait_ge(S.nm_ready, B + u + 1)
                        x = prob[0:LQ, u % 3, 0:LT]
                        nc.scalar.activation(x, x, ACT.Exp, scale=-1.0, bias=nmax[0:LQ, u % 3:u % 3 + 1],
                                             accum_out=denom[0:LQ, u % 3:u % 3 + 1]).then_inc(S.exp_ready, 1)

                    def applied(b, c):
                        act.wait_ge(S.u_mm, START + it * (NB * DC) + b * DC + c + 1)
                        dst = U[:, 0, c * HG * ROWS:(c + 1) * HG * ROWS]\
                            .rearrange("p (h n) -> p h n", h=HG)[:, :, b * LQ:(b + 1) * LQ]
                        high(dst, bank[6 + c % 2][:, 0:ROWS].rearrange("p (h n) -> p h n", h=HG))\
                            .then_inc(S.u_hi, 1)

                    for s in STEPS0:
                        if s < UNITS:
                            keys(s)
                        if s >= 2:
                            p_turned(s - 2)
                        if 1 <= s <= UNITS:
                            exponent(s - 1)
                        for b, c in APPLY.get(s, []):
                            applied(b, c)
                    for h in range(HG):
                        reached = act.to_reg(START + it * HG + h + 1)
                        act.wait_ge(S.cols_ready, 1)
                        act.wait_ge(S.v_tmp, reached)
                        if h >= 2:
                            act.wait_ge(S.w_done, done(n, T0["o", h - 2]))
                        high(part[:, h % 2, 0, :], tmp[:, h % 2, :], head_col("bv", h)).then_inc(S.v_hi, 1)

            def mlp_block(half, m):
                bias, gelu = mlp[m][2:]
                with act.Fori(0, MLP_STEPS) as st:
                    M, n = mlp_step(half, m, st)
                    for f in range(MLP_F):
                        reached = act.to_reg(done(n, TM["a", f]))
                        act.wait_ge(S.cols_ready, 1)
                        act.wait_ge(S.w_done, reached)
                        if f >= 2:
                            reached = act.to_reg(M * MLP_F + f - 1)
                            act.wait_ge(S.cols_ready, 1)
                            act.wait_ge(S.m_lo, reached)
                        nc.scalar.activation(tmp[:, f % 2, :], bank[f % 2][:, 0:ROWS], gelu,
                                             bias=cols[:, bass.ds(st * MLP_F + (col[bias] + f), 1)])\
                            .then_inc(S.m_gelu, 1)
                        act.wait_ge(S.m_gelu, START + M * MLP_F + f + 1)
                        high(part[:, f % 2, 0, :], tmp[:, f % 2, :]).then_inc(S.m_hi, 1)

            def attention1(half):
                n = half * HALF_TILES + ATT1_BASE
                act.wait_ge(S.qz_ready, (half + 1) * 2)
                for j in range(4):
                    act.wait_ge(S.w_done, done(n, T1["q", j]))
                    for i in range(HG):
                        r, a = slice(i * HD1, (i + 1) * HD1), (j * HG + i) * ROWS
                        high(q_masked[r, 0, a:a + ROWS], bank[j % 2][r, 0:ROWS],
                             cols[r, col["L1_xattn_q_b"] + j:col["L1_xattn_q_b"] + j + 1]).then_inc(S.q1_hi, 1)

                def values(b):
                    for t in range(TC):
                        if b == NB - 1 and t == TC - 1:
                            act.wait_ge(S.w_done, done(n, T1["v", 3]))
                        else:
                            act.wait_ge(S.v1_mm, half * (NB * TC - 1) + b * TC + t + 1)
                        high(v1[b % 2][0:TK[t], 0, t * D:(t + 1) * D], bank[6 + t % 2][0:TK[t], :])\
                            .then_inc(S.v1_hi, 1)

                def keys(s):
                    b, j = divmod(s, 4)
                    if b == NB - 1:
                        act.wait_ge(S.w_done, done(n, T1["k", j]))
                    else:
                        act.wait_ge(S.k1_mm, half * ((NB - 1) * 4) + s + 1)
                    high(kT[:, s % 2, 0, :], bank[s % 2][:, 0:LT],
                         cols[:, col["L1_xattn_k_b"] + j:col["L1_xattn_k_b"] + j + 1]).then_inc(S.k1_hi, 1)

                def p_turned(u):
                    s, i = divmod(u, HG)
                    act.wait_ge(S.t1_mm, START + half * U1 + u + 1)
                    dst = pT[:, s % 2, 0, :].rearrange("p (t n) -> p t n", t=TC)[:, :, i * LQ:(i + 1) * LQ]
                    high(dst, bank[4 + u % 2][:, 0:TC * LQ].rearrange("p (t n) -> p t n", t=TC))\
                        .then_inc(S.pt1_hi, 1)

                def exponent(u):
                    act.wait_ge(S.nm1_ready, START + half * U1 + u + 1)
                    x = prob[0:LQ, u % 3, 1:LT]
                    nc.scalar.activation(x, x, ACT.Exp, scale=-1.0, bias=nmax[0:LQ, u % 3:u % 3 + 1],
                                         accum_out=denom[0:LQ, u % 3:u % 3 + 1]).then_inc(S.exp1_ready, 1)

                def applied(s):
                    b, j = divmod(s, 4)
                    act.wait_ge(S.a_mm, half * G1 + s + 1)
                    for i in range(HG):
                        r, a = slice(i * HD1, (i + 1) * HD1), j * ROWS + b * LQ
                        high(attnT[r, 0, a:a + LQ], bank[6 + s % 2][r, i * LQ:(i + 1) * LQ],
                             cols[r, col["L1_xattn_v_b"] + j:col["L1_xattn_v_b"] + j + 1]).then_inc(S.a_hi, 1)

                for s in range(G1 + 2):
                    if s < G1:
                        if s % 4 == 0:
                            values(s // 4)
                        keys(s)
                    for i in range(HG):
                        u = (s - 1) * HG + i
                        if 0 <= u - 2 < U1:
                            p_turned(u - 2)
                        if 0 <= u < U1:
                            exponent(u)
                    if s >= 2:
                        applied(s - 2)

            with act.Fori(0, 2) as half:
                layer_norm(half, 0)
                attention0(half, 0)
                layer_norm(half, 1)
                attention0(half, 1)
                layer_norm(half, 2)
                mlp_block(half, 0)
                layer_norm(half, 3)
                attention1(half)
                layer_norm(half, 4)
                mlp_block(half, 1)

        @block.vector
        def _(dve):
            def low(dst, src, bias, hi):
                return nc.vector.scalar_tensor_tensor(out=dst, in0=src, scalar=bias, in1=f32(hi),
                                                      op0=ALU.add, op1=ALU.subtract)

            def rest(dst, src, hi):
                return nc.vector.tensor_tensor(dst, src, f32(hi), ALU.subtract)

            nc.vector.memset(big[:], 0.0).then_inc(S.raw_cleared, 1)
            nc.vector.memset(eps, EPS).then_inc(S.extra_a, 1)
            nc.vector.memset(mean_w[:], 1.0 / D).then_inc(S.mean_ready, 1)
            dve.wait_ge(S.cols_mm, ncol_tiles)
            nc.vector.tensor_copy(cols[:], bank[0][:, 0:ncol_tiles * P]).then_inc(S.cols_ready, 1)
            nc.vector.memset(prob[:], 0.0).then_inc(S.prob_cleared, 1)
            dve.wait_ge(S.cols_ready, 1)
            for layer in range(2):
                bk = col[f"L0_xattn_bias_k{layer + 1}"]
                bias_v, bv = col[f"L0_xattn_bias_v{layer + 1}"], col[f"L0_xattn_bv{layer + 1}"]
                nc.vector.tensor_copy(extra_k[:, layer, :, 0], cols[:, bk:bk + HEADS0]).then_inc(S.extra_a, 1)
                dve.wait_ge(S.extra_a, 2 + layer)
                nc.vector.tensor_tensor(extra_k[:, layer, :, 1], cols[:, bk:bk + HEADS0],
                                        f32(extra_k[:, layer, :, 0]), ALU.subtract).then_inc(S.extra_ready, 1)
                nc.vector.tensor_tensor(extra_v[:, layer, :], cols[:, bias_v:bias_v + HEADS0],
                                        cols[:, bv:bv + HEADS0], ALU.subtract).then_inc(S.extra_ready, 1)
            dve.wait_ge(S.extra_ready, 4)
            dve.wait_ge(S.prob_cleared, 1)

            with dve.Fori(0, BATCH // 2) as i:
                for b in range(2):
                    o = b * (U.shape[2] // 2)
                    dve.wait_ge(S.c_hi, START + i * (2 * (1 + DC)) + b * (1 + DC) + 1)
                    rest(by_chunk(U[:, 1, o:o + NAT]), raw_ctx[:, b].rearrange("p t (c k) -> p t c k", c=DC),
                         by_chunk(U[:, 0, o:o + NAT]))\
                        .then_inc(S.c_lo, 1)
                    for c in range(DC):
                        dve.wait_ge(S.c_hi, START + i * (2 * (1 + DC)) + b * (1 + DC) + c + 2)
                        a = o + NAT + c * LT
                        rest(U[:, 1, a:a + LT], bank[b * DC + c][:, 0:LT], U[:, 0, a:a + LT]).then_inc(S.c_lo, 1)

            def x_in(half):
                for b in range(NB):
                    dve.wait_ge(S.x_mm, START + half * NB + b + 1)
                    nc.vector.tensor_copy(xT[:, :, b * LQ:(b + 1) * LQ],
                                          bank[6 + b % 2][:, 0:DC * LQ].rearrange("p (c n) -> p c n", c=DC))\
                        .then_inc(S.x_ready, 1)

            def x_out(half):
                for b in range(NB):
                    dve.wait_ge(S.out_mm, half * NB + b + 1)
                    if b >= 2:
                        dve.wait_ge(S.out_saved[b % 2], START + half * 32 + 16)
                    nc.vector.tensor_copy(xio[0:LQ, b % 2, :], bank[6 + b % 2][0:LQ, :]).then_inc(S.out_copied, 1)

            def add_to_x(added):
                for c in range(DC):
                    nc.vector.tensor_tensor(xT[:, c, :], xT[:, c, :], bank[2 + c][:, 0:ROWS], ALU.add)\
                        .then_inc(added, 1)

            def layer_norm(half, l):
                li = half * NORMS + l
                scale, offset, bias = norms[l][:3]
                dve.wait_ge(S.ln_mm, li + 1)
                for c in range(DC):
                    nc.vector.tensor_tensor(centred[:, c, :], xT[:, c, :], bank[0][:, 0:ROWS], ALU.subtract)\
                        .then_inc(S.ln_cent, 1)
                dve.wait_ge(S.ln_std, li + 1)
                nc.vector.reciprocal(tmp[:, 1, :], tmp[:, 0, :]).then_inc(S.ln_rstd, 1)

                def scaled(c):
                    nc.vector.scalar_tensor_tensor(
                        out=centred[:, c, :], in0=centred[:, c, :], scalar=cols[:, col[scale] + c:col[scale] + c + 1],
                        in1=tmp[:, 1, :], op0=ALU.mult, op1=ALU.mult).then_inc(S.ln_y, 1)

                def split(c):
                    dve.wait_ge(S.ln_hi, li * DC + c + 1)
                    low(hT_c(1, c), centred[:, c, :], cols[:, col[offset] + c:col[offset] + c + 1], hT_c(0, c))\
                        .then_inc(S.ln_lo, 1)

                dve.wait_ge(S.ln_rstd, li + 1)
                dve.wait_ge(S.ln_cent, (li + 1) * DC)
                scaled(0)
                for c in range(1, DC):
                    scaled(c)
                    split(c - 1)
                split(DC - 1)
                for c in range(DC):
                    nc.vector.tensor_scalar(xT[:, c, :], xT[:, c, :], cols[:, col[bias] + c:col[bias] + c + 1], None,
                                            ALU.add).then_inc(S.ln_bias, 1)
                reached = dve.to_reg((li + 1) * DC)
                dve.wait_ge(S.cols_ready, 1)
                dve.wait_ge(S.ln_bias, reached)

            def attention0(half, layer):
                with dve.Fori(0, GROUPS) as g:
                    it, n = att0_step(half, layer, g)
                    B = it * UNITS

                    def head_col(name, h):
                        return cols[:, bass.ds(g * HG + (col[f"L0_xattn_{name}{layer + 1}"] + h), 1)]

                    for h in range(HG):
                        dve.wait_ge(S.q_hi, it * HG + h + 1)
                        low(qT[:, 1, h * ROWS:(h + 1) * ROWS], bank[h % 2][:, 0:ROWS], head_col("bq", h),
                            qT[:, 0, h * ROWS:(h + 1) * ROWS]).then_inc(S.q_lo, 1)

                    def keys(u):
                        b, h = divmod(u, HG)
                        dve.wait_ge(S.k_hi, B + u + 1)
                        nc.vector.tensor_scalar(kT[:, u % 2, :, 0],
                                                f32(extra_k[:, layer, bass.ds(g * HG + h, 1), :])
                                                .rearrange("p o n -> p (o n)"), 1.0, None, ALU.mult)\
                            .then_inc(S.k_col, 1)
                        low(kT[:, u % 2, 1, 1:LT], bank[u % 2][:, 1:LT], head_col("bk", h), kT[:, u % 2, 0, 1:LT])\
                            .then_inc(S.k_lo, 1)

                    def maximum(u):
                        dve.wait_ge(S.s_mm, B + u + 1)
                        dve.wait_ge(S.t_mm, START + B + max(u - 2, 0))
                        nc.vector.tensor_scalar(prob[0:LQ, u % 3, 0:LT], bank[2 + u % 2][0:LQ, 0:LT], -SCALE0, None,
                                                ALU.mult, ALU.min, accum_out=nmax[0:LQ, u % 3:u % 3 + 1])\
                            .then_inc(S.nm_ready, 1)

                    def normalise(u):
                        dve.wait_ge(S.exp_ready, B + u + 1)
                        d, r = denom[0:LQ, u % 3:u % 3 + 1], rden[0:LQ, u % 3:u % 3 + 1]
                        nc.vector.reciprocal(r, d).then_inc(S.rden_ready, 1)
                        dve.wait_ge(S.rden_ready, B + u + 1)
                        x = prob[0:LQ, u % 3, 0:LT]
                        nc.vector.tensor_scalar(x, x, r, None, ALU.mult).then_inc(S.p_ready, 1)

                    def p_turned(u):
                        b, h = divmod(u, HG)
                        dve.wait_ge(S.pt_hi, B + u + 1)
                        hi, lo = (pT[:, b % 2, p_, :].rearrange("p (t n) -> p t n", t=TC)[:, :, h * LQ:(h + 1) * LQ]
                                  for p_ in range(2))
                        rest(lo, bank[4 + u % 2][:, 0:TC * LQ].rearrange("p (t n) -> p t n", t=TC), hi)\
                            .then_inc(S.pt_lo, 1)

                    def applied(b, c):
                        dve.wait_ge(S.u_hi, it * (NB * DC) + b * DC + c + 1)
                        hi, lo = (U[:, p_, c * HG * ROWS:(c + 1) * HG * ROWS]
                                  .rearrange("p (h n) -> p h n", h=HG)[:, :, b * LQ:(b + 1) * LQ]
                                  for p_ in range(2))
                        rest(lo, bank[6 + c % 2][:, 0:ROWS].rearrange("p (h n) -> p h n", h=HG), hi)\
                            .then_inc(S.u_lo, 1)

                    for s in STEPS0:
                        if s < UNITS:
                            keys(s)
                        if 1 <= s <= UNITS:
                            maximum(s - 1)
                        if s >= 2:
                            p_turned(s - 2)
                        if 1 <= s <= UNITS:
                            normalise(s - 1)
                        for b, c in APPLY.get(s, []):
                            applied(b, c)

                    def value_sum(h):
                        dve.wait_ge(S.w_done, done(n, T0["v", h]))
                        if h == 0:
                            dve.wait_ge(S.p0_ready, START + (it + 1) * NB)
                        if h >= 2:
                            dve.wait_ge(S.v_lo, it * HG + h - 1)
                        nc.vector.scalar_tensor_tensor(
                            out=tmp[:, h % 2, :].rearrange("p (b n) -> p b n", b=NB),
                            in0=p0_all[:, :, h * LQ:(h + 1) * LQ],
                            scalar=extra_v[:, layer, bass.ds(g * HG + h, 1)],
                            in1=bank[6 + h % 2][:, 0:ROWS].rearrange("p (b n) -> p b n", b=NB),
                            op0=ALU.mult, op1=ALU.add).then_inc(S.v_tmp, 1)

                    def value_low(h):
                        dve.wait_ge(S.v_hi, it * HG + h + 1)
                        low(part[:, h % 2, 1, :], tmp[:, h % 2, :], head_col("bv", h), part[:, h % 2, 0, :])\
                            .then_inc(S.v_lo, 1)

                    value_sum(0)
                    for h in range(1, HG):
                        value_low(h - 1)
                        value_sum(h)
                    value_low(HG - 1)
                    dve.wait_ge(S.w_done, done(n, T0["o", HG - 1]))
                    dve.wait_ge(S.x_add, START + it * DC)
                    add_to_x(S.x_add)

            def mlp_block(half, m):
                with dve.Fori(0, MLP_STEPS) as st:
                    M, n = mlp_step(half, m, st)
                    for f in range(MLP_F):
                        dve.wait_ge(S.m_hi, M * MLP_F + f + 1)
                        rest(part[:, f % 2, 1, :], tmp[:, f % 2, :], part[:, f % 2, 0, :]).then_inc(S.m_lo, 1)
                    dve.wait_ge(S.w_done, done(n, TM["b", MLP_F - 1]))
                    dve.wait_ge(S.m_add, START + M * DC)
                    add_to_x(S.m_add)

            def attention1(half):
                n = half * HALF_TILES + ATT1_BASE
                nc.vector.memset(prob[0:LQ, :, 0:1], 0.0).then_inc(S.p1_cleared, 1)
                dve.wait_ge(S.p1_cleared, half + 1)
                for j in range(4):
                    for i in range(HG):
                        r, a = slice(i * HD1, (i + 1) * HD1), (j * HG + i) * ROWS
                        dve.wait_ge(S.q1_hi, half * 16 + j * HG + i + 1)
                        low(q_masked[r, 1, a:a + ROWS], bank[j % 2][r, 0:ROWS],
                            cols[r, col["L1_xattn_q_b"] + j:col["L1_xattn_q_b"] + j + 1],
                            q_masked[r, 0, a:a + ROWS]).then_inc(S.q1_lo, 1)

                def values(b):
                    for t in range(TC):
                        dve.wait_ge(S.v1_hi, half * (NB * TC) + b * TC + t + 1)
                        hi, lo = (v1[b % 2][0:TK[t], p_, t * D:(t + 1) * D] for p_ in range(2))
                        rest(lo, bank[6 + t % 2][0:TK[t], :], hi).then_inc(S.v1_lo, 1)

                def keys(s):
                    b, j = divmod(s, 4)
                    dve.wait_ge(S.k1_hi, half * G1 + s + 1)
                    low(kT[:, s % 2, 1, :], bank[s % 2][:, 0:LT],
                        cols[:, col["L1_xattn_k_b"] + j:col["L1_xattn_k_b"] + j + 1], kT[:, s % 2, 0, :])\
                        .then_inc(S.k1_lo, 1)

                def maximum(u):
                    b = u // HEADS0
                    reached = dve.to_reg(half * U1 + u + 1)
                    dve.wait_ge(S.cols_ready, 1)
                    dve.wait_ge(S.s1_mm, reached)
                    dve.wait_ge(S.t1_mm, START + half * U1 + max(u - 2, 0))
                    if u % HEADS0 == 0:
                        dve.wait_ge(S.mask_ready, START + half * NB + b + 1)
                    nc.vector.tensor_tensor_reduce(out=prob[0:LQ, u % 3, 1:LT], in0=bank[2 + u % 2][0:LQ, 1:LT],
                                                   in1=mask_off[0:LQ, b % 2, 1:LT], scale=-SCALE1, scalar=FMAX,
                                                   op0=ALU.add, op1=ALU.min, accum_out=nmax[0:LQ, u % 3:u % 3 + 1])\
                        .then_inc(S.nm1_ready, 1)

                def normalise(u):
                    dve.wait_ge(S.exp1_ready, half * U1 + u + 1)
                    d, r = denom[0:LQ, u % 3:u % 3 + 1], rden[0:LQ, u % 3:u % 3 + 1]
                    nc.vector.reciprocal(r, d).then_inc(S.rden1_ready, 1)
                    dve.wait_ge(S.rden1_ready, half * U1 + u + 1)
                    x = prob[0:LQ, u % 3, 1:LT]
                    nc.vector.tensor_scalar(x, x, r, None, ALU.mult).then_inc(S.p1_ready, 1)

                def p_turned(u):
                    s, i = divmod(u, HG)
                    dve.wait_ge(S.pt1_hi, half * U1 + u + 1)
                    hi, lo = (pT[:, s % 2, p_, :].rearrange("p (t n) -> p t n", t=TC)[:, :, i * LQ:(i + 1) * LQ]
                              for p_ in range(2))
                    rest(lo, bank[4 + u % 2][:, 0:TC * LQ].rearrange("p (t n) -> p t n", t=TC), hi)\
                        .then_inc(S.pt1_lo, 1)

                def applied(s):
                    b, j = divmod(s, 4)
                    for i in range(HG):
                        r, a = slice(i * HD1, (i + 1) * HD1), j * ROWS + b * LQ
                        dve.wait_ge(S.a_hi, half * (G1 * HG) + s * HG + i + 1)
                        low(attnT[r, 1, a:a + LQ], bank[6 + s % 2][r, i * LQ:(i + 1) * LQ],
                            cols[r, col["L1_xattn_v_b"] + j:col["L1_xattn_v_b"] + j + 1], attnT[r, 0, a:a + LQ])\
                            .then_inc(S.a_lo, 1)

                for s in range(G1 + 2):
                    if s < G1:
                        if s % 4 == 0:
                            values(s // 4)
                        keys(s)
                    for i in range(HG):
                        u = (s - 1) * HG + i
                        if 0 <= u < U1:
                            maximum(u)
                        if 0 <= u - 2 < U1:
                            p_turned(u - 2)
                        if 0 <= u < U1:
                            normalise(u)
                    if s >= 2:
                        applied(s - 2)
                dve.wait_ge(S.w_done, done(n, T1["c", 3]))
                add_to_x(S.c_add)

            with dve.Fori(0, 2) as half:
                x_in(half)
                layer_norm(half, 0)
                attention0(half, 0)
                layer_norm(half, 1)
                attention0(half, 1)
                layer_norm(half, 2)
                mlp_block(half, 0)
                layer_norm(half, 3)
                attention1(half)
                layer_norm(half, 4)
                mlp_block(half, 1)
                x_out(half)


_LAYER0 = [f"L0_xattn_{x}{n}" for n in (1, 2) for x in
           ("wq", "bq", "wk", "bk", "wv", "bv", "wo", "bo", "bias_k", "bias_v")]
_INS = ["x", "ctx_2048", "mask_BxS2_bf1", *_LAYER0,
        "L0_xattn_ln1_scale", "L0_xattn_ln1_offset", "L0_xattn_ln2_scale", "L0_xattn_ln2_offset",
        "L0_xattn_ln_mlp_scale", "L0_xattn_ln_mlp_offset",
        "L0_xattn_w_fc1", "L0_xattn_b_fc1", "L0_xattn_w_fc2", "L0_xattn_b_fc2",
        "L1_xattn_ln1_w", "L1_xattn_ln1_b", "L1_xattn_q_w", "L1_xattn_q_b", "L1_xattn_k_w", "L1_xattn_k_b",
        "L1_xattn_v_w", "L1_xattn_v_b", "L1_xattn_cproj_w", "L1_xattn_cproj_b", "L1_xattn_ln2_w",
        "L1_xattn_ln2_b", "L1_xattn_fc_w", "L1_xattn_fc_b", "L1_xattn_proj_w", "L1_xattn_proj_b"]


def kernel(**inputs):
    import numpy as _np
    import concourse.bacc as _bacc
    from concourse import mybir as _mybir
    from concourse.bass_utils import run_bass_kernel_spmd as _run

    nc = _bacc.Bacc("TRN2", target_bir_lowering=False, num_devices=1)
    arrays, tensors = {}, {}
    for name in _INS:
        a = _np.ascontiguousarray(inputs[name])
        if a.dtype.kind == "b":
            a = a.view(_np.uint8)
        arrays[f"in_{name}"] = a
        tensors[name] = nc.dram_tensor(f"in_{name}", a.shape, _mybir.dt.from_np(a.dtype), kind="ExternalInput").ap()
    out = nc.dram_tensor("out_0", (BATCH, LQ, D), F32, kind="ExternalOutput").ap()
    build(nc, tensors, out)
    r = _run(nc, [arrays], core_ids=[0])
    return r.results[0]["out_0"]
```

```python
from contextlib import ExitStack

import concourse.bass as bass
from concourse import mybir

ALU = mybir.AluOpType
ACT = mybir.ActivationFunctionType
F32 = mybir.dt.float32
F32R = mybir.dt.float32r
U8 = mybir.dt.uint8

P = 128
BATCH, LQ, LK, D = 8, 100, 361, 512
NB = BATCH // 2
ROWS = NB * LQ
LT = LK + 1
DC = D // P
TC = 3
TK = [P, P, LT - 2 * P]
HEADS0 = 16
INNER = HEADS0 * P
HG = 4
GROUPS = HEADS0 // HG
UNITS = NB * HG
HD1 = 32
RING = 8
STAGE = 4
PB = 4
LAG = 3
MLP_F = 8
MLP_STEPS = INNER // P // MLP_F
SCALE0 = float(P) ** -0.5
SCALE1 = float(HD1) ** -0.5
EPS = 1e-5
FMAX = 3.4028234663852886e38

ATT0_TILES = ([("q", h) for h in range(HG)] + [("k", h) for h in range(HG)]
              + [("v", 0), ("v", 1), ("v", 2), ("o", 0), ("v", 3), ("o", 1), ("o", 2), ("o", 3)])
MLP_TILES = [("a", 0)] + [t for f in range(1, MLP_F) for t in (("a", f), ("b", f - 1))] + [("b", MLP_F - 1)]
ATT1_TILES = [(m, j) for m in "qvkc" for j in range(4)]
HALF_TILES = 2 * GROUPS * len(ATT0_TILES) + 2 * MLP_STEPS * len(MLP_TILES) + len(ATT1_TILES)
ATT0_BASE = [0, GROUPS * len(ATT0_TILES)]
MLP_BASE = [2 * GROUPS * len(ATT0_TILES), HALF_TILES - MLP_STEPS * len(MLP_TILES)]
ATT1_BASE = MLP_BASE[1] - len(ATT1_TILES)
assert all(n % RING == 0 for n in (*ATT0_BASE, *MLP_BASE, ATT1_BASE, HALF_TILES))

COLUMNS = [
    [("L0_xattn_bq1", 16), ("L0_xattn_bk1", 16), ("L0_xattn_bv1", 16), ("L0_xattn_bias_k1", 16),
     ("L0_xattn_bias_v1", 16), ("L0_xattn_bo1", 4), ("L0_xattn_ln1_scale", 4), ("L0_xattn_ln1_offset", 4),
     ("L0_xattn_b_fc1", 16), ("L0_xattn_b_fc2", 4), ("L0_xattn_ln_mlp_scale", 4),
     ("L0_xattn_ln_mlp_offset", 4), ("L1_xattn_ln1_w", 4), ("L1_xattn_ln1_b", 4)],
    [("L0_xattn_bq2", 16), ("L0_xattn_bk2", 16), ("L0_xattn_bv2", 16), ("L0_xattn_bias_k2", 16),
     ("L0_xattn_bias_v2", 16), ("L0_xattn_bo2", 4), ("L0_xattn_ln2_scale", 4), ("L0_xattn_ln2_offset", 4),
     ("L1_xattn_fc_b", 16), ("L1_xattn_q_b", 4), ("L1_xattn_k_b", 4), ("L1_xattn_v_b", 4),
     ("L1_xattn_cproj_b", 4), ("L1_xattn_proj_b", 4)],
    [("L1_xattn_ln2_w", 4), ("L1_xattn_ln2_b", 4)],
]


def column_table():
    at = {}
    for t, group in enumerate(COLUMNS):
        n = t * P
        for name, rows in group:
            at[name] = n
            n += rows
        assert n <= (t + 1) * P
    return at


def build(nc, T, out):
    col = column_table()
    ncol_tiles = len(COLUMNS)
    col_dmas = sum(len(g) for g in COLUMNS)

    norms = [("L0_xattn_ln1_scale", "L0_xattn_ln1_offset", "L0_xattn_bo1", ACT.Exp),
             ("L0_xattn_ln2_scale", "L0_xattn_ln2_offset", "L0_xattn_bo2", ACT.Exp),
             ("L0_xattn_ln_mlp_scale", "L0_xattn_ln_mlp_offset", "L0_xattn_b_fc2", ACT.Gelu),
             ("L1_xattn_ln1_w", "L1_xattn_ln1_b", "L1_xattn_cproj_b", ACT.Exp),
             ("L1_xattn_ln2_w", "L1_xattn_ln2_b", "L1_xattn_proj_b", ACT.Gelu_apprx_tanh)]
    NORMS = len(norms)

    NAT, TRA = TC * D, DC * LT
    ctx_dram = nc.dram_tensor("ctx_parts", [BATCH, P, 2, NAT + TRA], F32, kind="Internal").ap()

    with ExitStack() as ctx:
        def sb(name, shape, dt):
            return ctx.enter_context(nc.sbuf_tensor(name, shape, dt))

        def sem(name):
            return ctx.enter_context(nc.semaphore(name))

        with nc.sbuf_tensor("raw_inputs", [P, 2 * NAT + NB * D], F32) as raw_inputs:
            raw_ctx = raw_inputs[:, 0:2 * NAT].rearrange("p (b t d) -> p b t d", b=2, t=TC)
            x_nat = raw_inputs[:, 2 * NAT:].rearrange("p (b d) -> p b d", b=NB)
        pT = sb("pT", [P, 2, 2, TC * ROWS], F32R)
        qT = sb("qT", [P, 2, HG * ROWS], F32R)
        big = sb("big", [P, 2 * ROWS * DC], F32)
        scratch = big[:, 0:DC * ROWS]
        xT = big[:, DC * ROWS:].rearrange("p (c n) -> p c n", c=DC)
        centred = scratch.rearrange("p (c n) -> p c n", c=DC)
        p0_all = scratch.rearrange("p (b n) -> p b n", b=NB)
        out_nat = scratch[:, 0:2 * D].rearrange("p (s d) -> p s d", s=2)
        mask01 = scratch[:, 0:2 * LT].rearrange("p (b n) -> p b n", b=2)
        mask_off = scratch[:, 2 * LT:4 * LT].rearrange("p (b n) -> p b n", b=2)
        hT = sb("hT", [P, 2, DC * ROWS], F32R)
        ring = sb("ring", [P, RING, 2, D], F32R)
        stage = sb("stage", [P, STAGE, D], F32)
        ctxT = sb("ctxT", [P, 2, 2, TRA], F32R)
        ctxN = sb("ctxN", [P, 2, NAT], F32R)
        kT = sb("kT", [P, 2, 2, LT], F32R)
        PW = TC * P
        prob = sb("prob", [P, PB, PW], F32)
        U = sb("U", [P, 2, DC * HG * ROWS], F32R)
        part = sb("part", [P, 2, 2, ROWS], F32R)
        tmp = sb("tmp", [P, 2, ROWS], F32)
        p0_row = sb("p0_row", [1, ROWS], F32)
        mask_u8 = sb("mask_u8", [P, 2, LK], U8)
        cols = sb("cols", [P, ncol_tiles * P], F32)
        extra_k = sb("extra_k", [P, 2, HEADS0, 2], F32R)
        extra_v = sb("extra_v", [P, 2, HEADS0], F32)
        ident = sb("ident", [P, P], F32)
        mean_w = sb("mean_w", [P, P], F32)
        stat = sb("stat", [P, 16], F32)
        nmax, denom, rden = (stat[:, k * PB:(k + 1) * PB] for k in range(3))
        eps, table_load = stat[:, 3 * PB:3 * PB + 1], stat[:, 3 * PB + 1:3 * PB + 3]
        q_masked = U
        attnT = qT
        v1 = [ctxN, hT]
        V1_BANK = [7, 1, 6]

        bank = [ctx.enter_context(nc.psum_tensor(f"bank{i}", [P, 512], F32)) for i in range(8)]

        class S:
            pass

        S.cols_in = sem("cols_in")
        S.cols_cleared = sem("cols_cleared")
        S.ident_cleared = sem("ident_cleared")
        S.ident_ready = sem("ident_ready")
        S.cols_mm = sem("cols_mm")
        S.cols_ready = sem("cols_ready")
        S.prob_cleared = sem("prob_cleared")
        S.mean_ready = sem("mean_ready")
        S.extra_a = sem("extra_a")
        S.extra_ready = sem("extra_ready")
        S.raw_cleared = sem("raw_cleared")
        S.c_mm = sem("c_mm")
        S.w_hi = sem("w_hi")
        S.w_ready = sem("w_ready")
        S.w_done = sem("w_done")
        S.x_mm = sem("x_mm")
        S.x_ready = sem("x_ready")
        S.out_mm = sem("out_mm")
        S.out_copied = sem("out_copied")
        S.ln_hi = sem("ln_hi")
        S.ln_lo = sem("ln_lo")
        S.ln_mm = sem("ln_mm")
        S.ln_var = sem("ln_var")
        S.ln_cent = sem("ln_cent")
        S.ln_sq = sem("ln_sq")
        S.ln_std = sem("ln_std")
        S.ln_rstd = sem("ln_rstd")
        S.ln_y = sem("ln_y")
        S.ln_bias = sem("ln_bias")
        S.q_hi = sem("q_hi")
        S.q_lo = sem("q_lo")
        S.k_mm = sem("k_mm")
        S.k_hi = sem("k_hi")
        S.k_lo = sem("k_lo")
        S.k_col = sem("k_col")
        S.s_mm = sem("s_mm")
        S.nm_ready = sem("nm_ready")
        S.exp_ready = sem("exp_ready")
        S.rden_ready = sem("rden_ready")
        S.p_ready = sem("p_ready")
        S.t_mm = sem("t_mm")
        S.pt_hi = sem("pt_hi")
        S.pt_lo = sem("pt_lo")
        S.u_mm = sem("u_mm")
        S.u_hi = sem("u_hi")
        S.u_lo = sem("u_lo")
        S.o_mm = sem("o_mm")
        S.v_tmp = sem("v_tmp")
        S.v_hi = sem("v_hi")
        S.v_lo = sem("v_lo")
        S.x_add = sem("x_add")
        S.p0_add = sem("p0_add")
        S.p0_ready = sem("p0_ready")
        S.m_mm = sem("m_mm")
        S.m_gelu = sem("m_gelu")
        S.m_hi = sem("m_hi")
        S.m_lo = sem("m_lo")
        S.m_add = sem("m_add")
        S.mask_a = sem("mask_a")
        S.mask_ready = sem("mask_ready")
        S.qz_ready = sem("qz_ready")
        S.q1_hi = sem("q1_hi")
        S.q1_lo = sem("q1_lo")
        S.k1_mm = sem("k1_mm")
        S.k1_hi = sem("k1_hi")
        S.k1_lo = sem("k1_lo")
        S.v1_mm = sem("v1_mm")
        S.v1_hi = sem("v1_hi")
        S.v1_lo = sem("v1_lo")
        S.s1_mm = sem("s1_mm")
        S.nm1_ready = sem("nm1_ready")
        S.exp1_ready = sem("exp1_ready")
        S.rden1_ready = sem("rden1_ready")
        S.p1_ready = sem("p1_ready")
        S.p1_act = sem("p1_act")
        S.t1_mm = sem("t1_mm")
        S.pt1_hi = sem("pt1_hi")
        S.pt1_lo = sem("pt1_lo")
        S.cproj_mm = sem("cproj_mm")
        S.a_mm = sem("a_mm")
        S.a_hi = sem("a_hi")
        S.a_lo = sem("a_lo")
        S.c_add = sem("c_add")
        S.p1_cleared = sem("p1_cleared")
        S.w_in = [sem(f"w_in{k}") for k in range(STAGE)]
        S.raw_in = [sem(f"raw_in{b}") for b in range(2)]
        S.c_hi = [sem(f"c_hi{b}") for b in range(2)]
        S.c_lo = [sem(f"c_lo{b}") for b in range(2)]
        S.c_out = [sem(f"c_out{b}") for b in range(2)]
        S.ctxT_in = [sem(f"ctxT_in{b}") for b in range(2)]
        S.ctxN_in = [sem(f"ctxN_in{c}") for c in range(DC)]
        S.x_in = [sem(f"x_in{b}") for b in range(NB)]
        S.out_saved = [sem(f"out_saved{b}") for b in range(2)]
        S.mask_in = [sem(f"mask_in{b}") for b in range(2)]
        START = 1

        def split_mms(eng, dst, parts_l, parts_r, first, last):
            order = [(0, 0), (0, 1), (1, 0)]
            for n, (a, b) in enumerate(order):
                mm = eng.matmul(dst, parts_l[a], parts_r[b], start=first and n == 0,
                                stop=last and n == len(order) - 1)
            return mm

        def f32(ap):
            return ap.bitcast(F32)

        def by_chunk(natural):
            return natural.rearrange("p (c t k) -> p t c k", c=DC, t=TC)

        def hT_c(part_, c):
            return hT[:, part_, c * ROWS:(c + 1) * ROWS]

        def w_slot(k):
            return [ring[:, k % RING, p_, :] for p_ in range(2)]

        def w_cols(k, c):
            return [w[:, c * P:(c + 1) * P] for w in w_slot(k)]

        def ctxT_c(buf, c, t0=0, t1=LT):
            return [ctxT[:, buf, p_, c * LT + t0:c * LT + t1] for p_ in range(2)]

        def two(t):
            return [t[:, p_] for p_ in range(2)]

        def att0_step(half, layer, g):
            it = half * (2 * GROUPS) + layer * GROUPS + g
            n = half * HALF_TILES + ATT0_BASE[layer] + g * len(ATT0_TILES)
            return it, n

        def mlp_step(half, m, st):
            M = half * (2 * MLP_STEPS) + m * MLP_STEPS + st
            n = half * HALF_TILES + MLP_BASE[m] + st * len(MLP_TILES)
            return M, n

        T0 = {t: k for k, t in enumerate(ATT0_TILES)}
        TM = {t: k for k, t in enumerate(MLP_TILES)}
        T1 = {t: k for k, t in enumerate(ATT1_TILES)}
        G1 = NB * 4
        U1 = NB * HEADS0

        def ready(n, k):
            return n + (STAGE + k + 1)

        def done(n, k):
            return START + n + (RING + k + 1)

        def by_act(u):
            return u % HG == 1

        L0 = [{k: T[f"L0_xattn_{k}{n}"] for k in ("wq", "wk", "wv", "wo")} for n in (1, 2)]
        mlp = [(T["L0_xattn_w_fc1"], T["L0_xattn_w_fc2"], "L0_xattn_b_fc1", ACT.Gelu),
               (T["L1_xattn_fc_w"], T["L1_xattn_proj_w"], "L1_xattn_fc_b", ACT.Gelu_apprx_tanh)]
        L1W = {"q": T["L1_xattn_q_w"], "k": T["L1_xattn_k_w"], "v": T["L1_xattn_v_w"], "c": T["L1_xattn_cproj_w"]}

        def column_tile(w, n):
            return w.rearrange("(c p) n -> p c n", p=P)[:, :, bass.ds(n * P, P)]

        def row_tile(w, n):
            return w.rearrange("(r p) n -> p r n", p=P)[:, bass.ds(n, 1), :]

        def x_complete(l, half, c):
            if l == 0:
                return S.x_ready, half * NB + NB
            if l in (1, 2):
                return S.x_add, START + (half * 2 + l) * (GROUPS * DC) - DC + c + 1
            if l == 3:
                return S.m_add, START + (half * 2 + 1) * (MLP_STEPS * DC) - DC + c + 1
            return S.c_add, START + half * DC + c + 1

        STEPS0 = range(UNITS + LAG)
        APPLY = {(b + 1) * HG + LAG: [(b, c) for c in range(DC)] for b in range(NB - 2)}
        APPLY[UNITS] = [(NB - 2, 0)]
        APPLY[UNITS + 1] = [(NB - 2, 1), (NB - 2, 2)]
        APPLY[UNITS + 2] = [(NB - 2, 3)] + [(NB - 1, c) for c in range(DC)]

        block = ctx.enter_context(nc.Block())

        @block.sync
        def _(sp):
            for semaphore in (*S.c_hi, *S.c_lo, *S.c_out, S.x_mm, S.x_add, S.k_mm, S.u_mm, S.v_tmp, S.p0_ready, S.t_mm,
                              S.m_gelu, S.m_add, S.c_add, *S.out_saved, S.out_copied, S.mask_ready, S.nm1_ready,
                              S.pt1_lo, S.a_lo, S.t1_mm):
                sp.sem_inc(semaphore, START)
            def load_context(i, b):
                src = T["ctx_2048"][bass.ds(i * 2 + b, 1)].rearrange("o t d -> (o t) d")
                for t in range(TC):
                    lo, hi = max(0, t * P - 1), min(LK, (t + 1) * P - 1)
                    r0 = 1 if t == 0 else 0
                    sp.dma_start(raw_ctx[r0:r0 + hi - lo, b, t, :], src[lo:hi, :]).then_inc(S.raw_in[b], 16)

            sp.wait_ge(S.raw_cleared, 1)
            with sp.Fori(0, BATCH // 2) as i:
                for b in range(2):
                    reached = sp.to_reg(START + i * (1 + DC))
                    sp.wait_ge(S.raw_cleared, 1)
                    sp.wait_ge(S.c_hi[b], reached)
                    sp.wait_ge(S.c_lo[b], reached)
                    load_context(i, b)

            def load_tile(n, k, src):
                reached = sp.to_reg(n + k + 1)
                sp.wait_ge(S.cols_ready, 1)
                sp.wait_ge(S.w_ready, reached)
                dst = stage[:, k % STAGE, :]
                if src.shape[1] == DC:
                    dst = dst.rearrange("p (c n) -> p c n", c=DC)
                else:
                    dst = dst.rearrange("p (r n) -> p r n", r=1)
                sp.dma_start(dst, src).then_inc(S.w_in[k % STAGE], 16)

            def load_ctxT(half, b, buf):
                sp.dma_start(f32(ctxT[:, buf]), ctx_dram[bass.ds(half * NB + b, 1), :, :, NAT:NAT + TRA]
                             .rearrange("o p s n -> p (o s) n")).then_inc(S.ctxT_in[buf], 16)

            def load_ctxN(half, b, c):
                sp.dma_start(f32(ctxN[:, :, c * PW:(c + 1) * PW]),
                             ctx_dram[bass.ds(half * NB + b, 1), :, :, c * PW:(c + 1) * PW]
                             .rearrange("o p s n -> p (o s) n")).then_inc(S.ctxN_in[c], 16)

            def attention0(half, layer):
                w = L0[layer]
                with sp.Fori(0, GROUPS) as g:
                    it, n = att0_step(half, layer, g)

                    def load_tiles(ks):
                        for k in ks:
                            m, h = ATT0_TILES[k]
                            src = w["w" + m]
                            load_tile(n, k, row_tile(src, g * HG + h) if m == "o" else column_tile(src, g * HG + h))

                    load_tiles(range(0, HG))
                    for b in range(2):
                        sp.wait_ge(S.c_out[b], START + 32 * (BATCH // 2))
                    reached = sp.to_reg(START + it * ((NB - 1) * HG))
                    sp.wait_ge(S.cols_ready, 1)
                    sp.wait_ge(S.k_mm, reached)
                    load_ctxT(half, 0, 0)
                    reached = sp.to_reg(START + n)
                    sp.wait_ge(S.cols_ready, 1)
                    sp.wait_ge(S.w_done, reached)
                    load_ctxT(half, 1, 1)
                    load_tiles(range(HG, RING))
                    reached = sp.to_reg(START + it * (NB * DC))
                    sp.wait_ge(S.cols_ready, 1)
                    sp.wait_ge(S.u_mm, reached)
                    for c in range(DC):
                        load_ctxN(half, 0, c)
                    load_tiles(range(RING, len(ATT0_TILES)))
                    for b in range(1, NB):
                        if b + 1 < NB:
                            reached = sp.to_reg(START + it * ((NB - 1) * HG) + b * HG)
                            sp.wait_ge(S.cols_ready, 1)
                            sp.wait_ge(S.k_mm, reached)
                            load_ctxT(half, b + 1, (b + 1) % 2)
                        for c in range(DC):
                            reached = sp.to_reg(START + it * (NB * DC) + (b - 1) * DC + c + 1)
                            sp.wait_ge(S.cols_ready, 1)
                            sp.wait_ge(S.u_mm, reached)
                            load_ctxN(half, b, c)

            def mlp_loads(half, m):
                wa, wb = mlp[m][:2]
                with sp.Fori(0, MLP_STEPS) as st:
                    _, n = mlp_step(half, m, st)
                    for k, (kind, f) in enumerate(MLP_TILES):
                        load_tile(n, k, (column_tile(wa, st * MLP_F + f) if kind == "a"
                                         else row_tile(wb, st * MLP_F + f)))

            with sp.Fori(0, 2) as half:
                reached = sp.to_reg(START + half * DC)
                sp.wait_ge(S.raw_cleared, 1)
                sp.wait_ge(S.c_add, reached)
                for b in range(NB):
                    sp.dma_start(x_nat[0:LQ, b, :], T["x"][bass.ds(half * NB + b, 1)]
                                 .rearrange("o q d -> (o q) d")).then_inc(S.x_in[b], 16)
                attention0(half, 0)
                attention0(half, 1)
                mlp_loads(half, 0)

                n = half * HALF_TILES + ATT1_BASE

                def load_mask(b):
                    sp.dma_start(mask_u8[0:LQ, b % 2, :], T["mask_BxS2_bf1"][bass.ds(half * NB + b, 1), :]
                                 .broadcast_to([LQ, LK])).then_inc(S.mask_in[b % 2], 16)

                last_group = half * HALF_TILES + (ATT0_BASE[1] + (GROUPS - 1) * len(ATT0_TILES))
                reached = sp.to_reg(done(last_group, RING - 1))
                sp.wait_ge(S.cols_ready, 1)
                sp.wait_ge(S.w_done, reached)
                load_ctxT(half, 0, 0)
                load_ctxT(half, 1, 1)
                reached = sp.to_reg(START + half * NB)
                sp.wait_ge(S.cols_ready, 1)
                sp.wait_ge(S.mask_ready, reached)
                load_mask(0)
                load_mask(1)
                for k, (m, j) in enumerate(ATT1_TILES):
                    if m == "c" and j == 0:
                        for b in range(2, NB):
                            reached = sp.to_reg(START + half * NB + b - 1)
                            sp.wait_ge(S.cols_ready, 1)
                            sp.wait_ge(S.mask_ready, reached)
                            load_mask(b)
                            reached = sp.to_reg(half * ((NB - 1) * 4) + (b - 1) * 4)
                            sp.wait_ge(S.cols_ready, 1)
                            sp.wait_ge(S.k1_mm, reached)
                            load_ctxT(half, b, b % 2)
                    load_tile(n, k, column_tile(L1W[m], j) if m in "qk" else row_tile(L1W[m], j))
                mlp_loads(half, 1)
            sp.wait_ge(S.out_saved[0], START + 64)
            sp.wait_ge(S.out_saved[1], START + 64)

        @block.gpsimd
        def _(pool):
            pool.sem_inc(S.w_ready, STAGE)
            nc.gpsimd.memset(prob[:], 0.0).then_inc(S.cols_cleared, 1)
            nc.gpsimd.memset(ident[:], 0.0).then_inc(S.ident_cleared, 1)
            pool.wait_ge(S.ident_cleared, 1)
            nc.gpsimd.affine_select(out=ident[:], in_=ident[:], compare_op=ALU.not_equal, fill=1.0, base=0,
                                    pattern=[[-1, P]], channel_multiplier=1).then_inc(S.ident_ready, 1)

            pool.wait_ge(S.cols_cleared, 1)
            for t, group in enumerate(COLUMNS):
                n = 0
                for name, rows in group:
                    src = T[name]
                    if len(src.shape) == 4:
                        src = src.rearrange("a b h k -> (a b h) k")
                    else:
                        src = src.rearrange("(r k) -> r k", k=P)
                    pool.dma_start(prob[n:n + rows, 0, t * P:(t + 1) * P], src).then_inc(S.cols_in, 16)
                    n += rows

            def split_tile(n, k):
                src, (hi, lo) = stage[:, k % STAGE, :], w_slot(k)
                pool.wait_ge(S.w_in[k % STAGE], n * 4 + ((k // STAGE) * 16 + 16))
                reached = pool.to_reg(START + n + k + 1)
                pool.wait_ge(S.cols_ready, 1)
                pool.wait_ge(S.w_done, reached)
                nc.gpsimd.tensor_scalar(hi, src, 1.0, 1.0, ALU.mult, ALU.mult).then_inc(S.w_hi, 1)
                pool.wait_ge(S.w_hi, n + k + 1)
                nc.gpsimd.tensor_tensor(lo, src, f32(hi), ALU.subtract).then_inc(S.w_ready, 1)

            def spread_p0(it, b):
                row0 = [f32(pT[0:1, b % 2, p_, 0:ROWS]) for p_ in range(2)]
                pool.wait_ge(S.pt_hi, it * UNITS + (b + 1) * HG)
                pool.wait_ge(S.pt_lo, it * UNITS + (b + 1) * HG)
                pool.wait_ge(S.p0_ready, START + it * NB + b)
                nc.gpsimd.tensor_tensor(p0_row[:], row0[0], row0[1], ALU.add).then_inc(S.p0_add, 1)
                reached = pool.to_reg(it * NB + b + 1)
                pool.wait_ge(S.cols_ready, 1)
                pool.wait_ge(S.p0_add, reached)
                pool.wait_ge(S.v_tmp, START + it * HG)
                nc.gpsimd.partition_broadcast(p0_all[:, b, :], p0_row[:], P).then_inc(S.p0_ready, 1)

            def attention0(half, layer):
                with pool.Fori(0, GROUPS) as g:
                    it, n = att0_step(half, layer, g)
                    for k in range(12):
                        split_tile(n, k)
                    for b in range(NB - 1):
                        spread_p0(it, b)
                    for k in range(12, 16):
                        split_tile(n, k)
                    spread_p0(it, NB - 1)

            def mlp_tiles(half, m):
                with pool.Fori(0, MLP_STEPS) as st:
                    _, n = mlp_step(half, m, st)
                    for k in range(len(MLP_TILES)):
                        split_tile(n, k)

            with pool.Fori(0, 2) as half:
                attention0(half, 0)
                attention0(half, 1)
                mlp_tiles(half, 0)
                reached = pool.to_reg(START + (half + 1) * (2 * GROUPS * DC))
                pool.wait_ge(S.cols_ready, 1)
                pool.wait_ge(S.x_add, reached)
                for p_ in range(2):
                    nc.gpsimd.memset(f32(q_masked[:, p_, :]), 0.0).then_inc(S.qz_ready, 1)
                n = half * HALF_TILES + ATT1_BASE
                for k in range(8):
                    split_tile(n, k)
                pool.wait_ge(S.ln_hi, (half * NORMS + 4) * DC)
                pool.wait_ge(S.ln_lo, (half * NORMS + 4) * DC)

                def convert_mask(b):
                    if b >= 2:
                        reached = pool.to_reg(START + half * U1 + (b - 1) * HEADS0)
                        pool.wait_ge(S.cols_ready, 1)
                        pool.wait_ge(S.nm1_ready, reached)
                    reached = pool.to_reg(half * 32 + (b // 2 + 1) * 16)
                    pool.wait_ge(S.cols_ready, 1)
                    pool.wait_ge(S.mask_in[b % 2], reached)
                    nc.gpsimd.tensor_scalar(mask01[0:LQ, b % 2, 1:LT], mask_u8[0:LQ, b % 2, :], 1.0, 1.0,
                                            ALU.mult, ALU.mult).then_inc(S.mask_a, 1)
                    reached = pool.to_reg(half * NB + b + 1)
                    pool.wait_ge(S.cols_ready, 1)
                    pool.wait_ge(S.mask_a, reached)
                    nc.gpsimd.tensor_scalar(mask_off[0:LQ, b % 2, 1:LT], mask01[0:LQ, b % 2, 1:LT], -1.0, FMAX,
                                            ALU.add, ALU.mult).then_inc(S.mask_ready, 1)

                convert_mask(0)
                convert_mask(1)
                for k in range(8, 12):
                    split_tile(n, k)
                convert_mask(2)
                convert_mask(3)
                for k in range(12, 16):
                    split_tile(n, k)
                mlp_tiles(half, 1)

        @block.tensor
        def _(pe):
            pe.sem_inc(S.w_done, START + RING)
            pe.wait_ge(S.ident_ready, 1)

            def turn_context(i):
                for b in range(2):
                    pe.wait_ge(S.raw_in[b], i * (16 * TC) + 16 * TC)
                    pe.wait_ge(S.c_hi[b], START + i * (1 + DC))
                    pe.wait_ge(S.c_lo[b], START + i * (1 + DC))
                    for c in range(DC):
                        for t in range(TC):
                            mm = pe.transpose(bank[b * DC + c][:, t * P:t * P + TK[t]],
                                              raw_ctx[0:TK[t], b, t, c * P:(c + 1) * P],
                                              ident[0:TK[t], 0:TK[t]])
                        mm.then_inc(S.c_mm, 1)

            with pe.Fori(0, BATCH // 2) as i:
                turn_context(i)
            for b in range(2):
                pe.wait_ge(S.c_hi[b], START + BATCH // 2 * (1 + DC))
                pe.wait_ge(S.c_lo[b], START + BATCH // 2 * (1 + DC))
            pe.wait_ge(S.cols_in, 16 * col_dmas)
            for t in range(ncol_tiles):
                pe.transpose(bank[0][:, t * P:(t + 1) * P], prob[:, 0, t * P:(t + 1) * P], ident[:])\
                  .then_inc(S.cols_mm, 1)
            pe.wait_ge(S.cols_ready, 1)
            pe.wait_ge(S.mean_ready, 1)

            def x_in(half):
                for b in range(NB):
                    pe.wait_ge(S.x_in[b], half * 16 + 16)
                    if b >= 2:
                        pe.wait_ge(S.out_copied, START + half * NB)
                    for c in range(DC):
                        mm = pe.transpose(bank[4 + b][:, c * LQ:(c + 1) * LQ],
                                          x_nat[0:LQ, b, c * P:(c + 1) * P], ident[0:LQ, 0:LQ])
                    mm.then_inc(S.x_mm, 1)

            def x_out(half):
                pe.wait_ge(S.m_add, START + (half + 1) * (2 * MLP_STEPS * DC))
                for b in range(NB):
                    if b >= 2:
                        pe.wait_ge(S.out_copied, START + half * NB + b - 1)
                    for c in range(DC):
                        mm = pe.transpose(bank[6 + b % 2][0:LQ, c * P:(c + 1) * P],
                                          xT[:, c, b * LQ:(b + 1) * LQ], ident[:])
                    mm.then_inc(S.out_mm, 1)

            def layer_norm(half, l):
                li = half * NORMS + l
                for c in range(DC):
                    pe.wait_ge(*x_complete(l, half, c))
                    mm = pe.matmul(bank[0][:, 0:ROWS], mean_w[:], xT[:, c, :], start=c == 0, stop=c == DC - 1)
                mm.then_inc(S.ln_mm, 1)
                for c in range(DC):
                    pe.wait_ge(S.ln_sq, li * DC + c + 1)
                    pe.matmul(bank[1][:, 0:ROWS], mean_w[:], tmp[:, c % 2, :], start=c == 0, stop=c == DC - 1)\
                      .then_inc(S.ln_var, 1)

            def norm_ready(half, l, c):
                pe.wait_ge(S.ln_hi, (half * NORMS + l) * DC + c + 1)
                pe.wait_ge(S.ln_lo, (half * NORMS + l) * DC + c + 1)

            def attention0(half, layer):
                with pe.Fori(0, GROUPS) as g:
                    it, n = att0_step(half, layer, g)
                    B = it * UNITS
                    for h in range(HG):
                        pe.wait_ge(S.w_ready, ready(n, T0["q", h]))
                        if h >= 2:
                            pe.wait_ge(S.q_lo, it * HG + h - 1)
                        for c in range(DC):
                            if h == 0:
                                norm_ready(half, layer, c)
                            mm = split_mms(pe, bank[h % 2][:, 0:ROWS], w_cols(T0["q", h], c),
                                           [hT_c(0, c), hT_c(1, c)], c == 0, c == DC - 1)
                        mm.then_inc(S.w_done, 1)

                    def keys(u):
                        b, h = divmod(u, HG)
                        if b == 0:
                            pe.wait_ge(S.w_ready, ready(n, T0["k", h]))
                        if h == 0:
                            pe.wait_ge(S.ctxT_in[b % 2], half * (18 * 16) + (layer * 8 + b // 2 + 1) * 16 + g * 32)
                        if u < 2:
                            pe.wait_ge(S.q_lo, it * HG + 3 + u)
                        else:
                            pe.wait_ge(S.k_lo, B + u - 1)
                        for c in range(DC):
                            mm = split_mms(pe, bank[u % 2][:, 0:LT], w_cols(T0["k", h], c),
                                           ctxT_c(b % 2, c), c == 0, c == DC - 1)
                        mm.then_inc(S.w_done if b == NB - 1 else S.k_mm, 1)

                    def logits(u):
                        b, h = divmod(u, HG)
                        pe.wait_ge(S.k_hi, B + u + 1)
                        pe.wait_ge(S.k_lo, B + u + 1)
                        pe.wait_ge(S.k_col, B + u + 1)
                        if u == 0:
                            pe.wait_ge(S.q_hi, it * HG + HG)
                            pe.wait_ge(S.x_add, START + it * DC)
                        if u >= 2:
                            pe.wait_ge(S.nm_ready, B + u - 1)
                        a = h * ROWS + b * LQ
                        split_mms(pe, bank[2 + u % 2][0:LQ, 0:LT], [qT[:, p_, a:a + LQ] for p_ in range(2)],
                                  [kT[:, u % 2, p_, :] for p_ in range(2)], True, True).then_inc(S.s_mm, 1)

                    def transpose_p(u):
                        pe.wait_ge(S.p_ready, B + u + 1)
                        if u >= 2:
                            pe.wait_ge(S.pt_lo, B + u - 1)
                        for t in range(TC):
                            mm = pe.transpose(bank[4 + u % 2][:, t * LQ:(t + 1) * LQ],
                                              prob[0:LQ, u % PB, t * P:(t + 1) * P], ident[0:LQ, 0:LQ])
                        mm.then_inc(S.t_mm, 1)

                    def apply_p(b, c):
                        if c == 0:
                            pe.wait_ge(S.pt_hi, B + (b + 1) * HG)
                            pe.wait_ge(S.pt_lo, B + (b + 1) * HG)
                        pe.wait_ge(S.ctxN_in[c], half * (32 * 16) + (layer * 16 + b + 1) * 16 + g * (NB * 16))
                        m = b * DC + c
                        if m < 2:
                            pe.wait_ge(S.v_tmp, START + it * HG)
                        else:
                            pe.wait_ge(S.u_lo, it * (NB * DC) + m - 1)
                        for t in range(TC):
                            K = TK[t]
                            mm = split_mms(pe, bank[6 + c % 2][:, 0:ROWS],
                                           [ctxN[0:K, p_, (c * TC + t) * P:(c * TC + t + 1) * P] for p_ in range(2)],
                                           [pT[0:K, b % 2, p_, t * ROWS:(t + 1) * ROWS] for p_ in range(2)],
                                           t == 0, t == TC - 1)
                        mm.then_inc(S.u_mm, 1)

                    def values(h):
                        pe.wait_ge(S.w_ready, ready(n, T0["v", h]))
                        if h >= 2:
                            pe.wait_ge(S.v_tmp, START + it * HG + h - 1)
                        for c in range(DC):
                            if h == 0 and c in (0, DC - 1):
                                chunks = (NB - 1) * DC + (DC - 1 if c == 0 else DC)
                                pe.wait_ge(S.u_hi, it * (NB * DC) + chunks)
                                pe.wait_ge(S.u_lo, it * (NB * DC) + chunks)
                            a = (c * HG + h) * ROWS
                            mm = split_mms(pe, bank[6 + h % 2][:, 0:ROWS], w_cols(T0["v", h], c),
                                           [U[:, p_, a:a + ROWS] for p_ in range(2)], c == 0, c == DC - 1)
                        mm.then_inc(S.w_done, 1)

                    def project(h):
                        pe.wait_ge(S.w_ready, ready(n, T0["o", h]))
                        pe.wait_ge(S.v_hi, it * HG + h + 1)
                        pe.wait_ge(S.v_lo, it * HG + h + 1)
                        w = w_slot(T0["o", h])
                        for c in range(DC):
                            mm = split_mms(pe, bank[2 + c][:, 0:ROWS], [x[:, c * P:(c + 1) * P] for x in w],
                                           [part[:, h % 2, p_, :] for p_ in range(2)], h == 0, h == HG - 1)
                            if h == HG - 1 and c < DC - 1:
                                mm.then_inc(S.o_mm, 1)
                        mm.then_inc(S.w_done, 1)

                    for s in STEPS0:
                        if s < UNITS:
                            keys(s)
                        if 1 <= s < UNITS:
                            logits(s - 1)
                        if s >= LAG:
                            transpose_p(s - LAG)
                        for b, c in APPLY.get(s, []):
                            apply_p(b, c)
                        if s == UNITS:
                            logits(s - 1)
                    for k in range(RING, len(ATT0_TILES)):
                        m, h = ATT0_TILES[k]
                        (values if m == "v" else project)(h)

            def mlp_block(half, m):
                with pe.Fori(0, MLP_STEPS) as st:
                    M, n = mlp_step(half, m, st)

                    def up(f):
                        pe.wait_ge(S.m_gelu, START + M * MLP_F + max(f - 1, 0))
                        for c in range(DC):
                            if f == 0:
                                norm_ready(half, 2 * m + 2, c)
                            mm = split_mms(pe, bank[f % 2][:, 0:ROWS], w_cols(TM["a", f], c),
                                           [hT_c(0, c), hT_c(1, c)], c == 0, c == DC - 1)
                        return mm

                    def down(f):
                        pe.wait_ge(S.m_hi, M * MLP_F + f + 1)
                        pe.wait_ge(S.m_lo, M * MLP_F + f + 1)
                        if f == 0:
                            pe.wait_ge(S.m_add, START + M * DC)
                        w = w_slot(TM["b", f])
                        for c in range(DC):
                            mm = split_mms(pe, bank[2 + c][:, 0:ROWS], [x[:, c * P:(c + 1) * P] for x in w],
                                           [part[:, f % 2, p_, :] for p_ in range(2)], f == 0, f == MLP_F - 1)
                            if f == MLP_F - 1 and c < DC - 1:
                                mm.then_inc(S.m_mm, 1)
                        return mm

                    for k, (kind, f) in enumerate(MLP_TILES):
                        pe.wait_ge(S.w_ready, ready(n, k))
                        (up if kind == "a" else down)(f).then_inc(S.w_done, 1)

            def attention1(half):
                n = half * HALF_TILES + ATT1_BASE
                for j in range(4):
                    pe.wait_ge(S.w_ready, ready(n, T1["q", j]))
                    if j >= 2:
                        pe.wait_ge(S.q1_lo, half * 16 + (j - 1) * HG)
                    for c in range(DC):
                        if j == 0:
                            norm_ready(half, 3, c)
                        mm = split_mms(pe, bank[j % 2][:, 0:ROWS], w_cols(T1["q", j], c),
                                       [hT_c(0, c), hT_c(1, c)], c == 0, c == DC - 1)
                    mm.then_inc(S.w_done, 1)

                def values(b):
                    if b == 0:
                        for j in range(4):
                            pe.wait_ge(S.w_ready, ready(n, T1["v", j]))
                    pe.wait_ge(S.ctxT_in[b % 2], half * (18 * 16) + (17 + b // 2) * 16)
                    for t in range(TC):
                        if b and t != 1:
                            pe.wait_ge(S.a_lo, START + half * (G1 * HG) + (4 * b - 4 + t // 2) * HG)
                        elif b:
                            pe.wait_ge(S.k1_lo, half * G1 + 4 * b)
                        elif t == 1:
                            pe.wait_ge(S.q1_lo, half * 16 + 16)
                        last_use = b == NB - 1 and t == TC - 1
                        for c in range(DC):
                            mm = split_mms(pe, bank[V1_BANK[t]][0:TK[t], :], ctxT_c(b % 2, c, t * P, t * P + TK[t]),
                                           w_slot(T1["v", c]), c == 0, c == DC - 1)
                            if last_use:
                                mm.then_inc(S.w_done, 1)
                        if not last_use:
                            mm.then_inc(S.v1_mm, 1)

                def keys(s, chunks):
                    b, j = divmod(s, 4)
                    if chunks[0] == 0:
                        if b == 0:
                            pe.wait_ge(S.w_ready, ready(n, T1["k", j]))
                        if s < 2:
                            pe.wait_ge(S.q1_lo, half * 16 + 16)
                        else:
                            pe.wait_ge(S.k1_lo, half * G1 + s - 1)
                        if j == 1:
                            pe.wait_ge(S.v1_lo, half * (NB * TC) + b * TC + 2)
                    for c in chunks:
                        mm = split_mms(pe, bank[s % 2][:, 0:LT], w_cols(T1["k", j], c), ctxT_c(b % 2, c),
                                       c == 0, c == DC - 1)
                    if c == DC - 1:
                        mm.then_inc(S.w_done if b == NB - 1 else S.k1_mm, 1)

                def logits(u):
                    s, i = divmod(u, HG)
                    b, j = divmod(s, 4)
                    pe.wait_ge(S.k1_hi, half * G1 + s + 1)
                    pe.wait_ge(S.k1_lo, half * G1 + s + 1)
                    pe.wait_ge(S.nm1_ready, START + half * U1 + max(u - 1, 0))
                    a = (j * HG + i) * ROWS + b * LQ
                    split_mms(pe, bank[2 + u % 2][0:LQ, 0:LT], [q_masked[:, p_, a:a + LQ] for p_ in range(2)],
                              [kT[:, s % 2, p_, :] for p_ in range(2)], True, True).then_inc(S.s1_mm, 1)

                def transpose_p(u):
                    if by_act(u):
                        pe.wait_ge(S.p1_act, half * G1 + u // HG + 1)
                    else:
                        pe.wait_ge(S.p1_ready, half * (U1 - G1) + u + 1 - (u + HG - 1) // HG)
                    pe.wait_ge(S.pt1_lo, START + half * U1 + max(u - 1, 0))
                    for t in range(TC):
                        mm = pe.transpose(bank[4 + u % 2][:, t * LQ:(t + 1) * LQ],
                                          prob[0:LQ, u % PB, t * P:(t + 1) * P], ident[0:LQ, 0:LQ])
                    mm.then_inc(S.t1_mm, 1)

                def apply_p(s, t):
                    b, j = divmod(s, 4)
                    vb, K = v1[b % 2], TK[t]
                    if t == 0:
                        pe.wait_ge(S.pt1_hi, half * U1 + (s + 1) * HG)
                        pe.wait_ge(S.pt1_lo, START + half * U1 + (s + 1) * HG)
                        later = min((s + 3) // 4, NB - 1)
                        seen = later * TC + 1 if later > b and j == 1 else (later + 1) * TC
                        pe.wait_ge(S.v1_hi, half * (NB * TC) + seen)
                        pe.wait_ge(S.v1_lo, half * (NB * TC) + seen)
                        pe.wait_ge(S.a_lo, START + half * (G1 * HG) + max(s - 1, 0) * HG)
                    mm = split_mms(pe, bank[6 + s % 2][:, 0:ROWS],
                                   [vb[0:K, p_, t * D + j * P:t * D + (j + 1) * P] for p_ in range(2)],
                                   [pT[0:K, s % 2, p_, t * ROWS:(t + 1) * ROWS] for p_ in range(2)],
                                   t == 0, t == TC - 1)
                    if t == TC - 1:
                        mm.then_inc(S.a_mm, 1)

                KEYS = [[0, 1], [2, 3], [], []]
                APPLIED = [[], [], [0, 1], [2]]
                for s in range(G1 + 3):
                    if s < G1 and s % 4 == 0:
                        values(s // 4)
                    for i in range(HG):
                        u = (s - 1) * HG + i
                        if 0 <= u < U1:
                            logits(u)
                        if s < G1 and KEYS[i]:
                            keys(s, KEYS[i])
                        if s >= 3:
                            for t in APPLIED[i]:
                                apply_p(s - 3, t)
                        if 0 <= u - LAG < U1:
                            transpose_p(u - LAG)
                pe.wait_ge(S.a_hi, (half + 1) * (G1 * HG))
                pe.wait_ge(S.a_lo, START + (half + 1) * (G1 * HG))
                for j in range(4):
                    pe.wait_ge(S.w_ready, ready(n, T1["c", j]))
                    w = w_slot(T1["c", j])
                    for c in range(DC):
                        mm = split_mms(pe, bank[2 + c][:, 0:ROWS], [x[:, c * P:(c + 1) * P] for x in w],
                                       [attnT[:, p_, j * ROWS:(j + 1) * ROWS] for p_ in range(2)], j == 0, j == 3)
                        if j == 3 and c < DC - 1:
                            mm.then_inc(S.cproj_mm, 1)
                    mm.then_inc(S.w_done, 1)

            with pe.Fori(0, 2) as half:
                x_in(half)
                layer_norm(half, 0)
                attention0(half, 0)
                layer_norm(half, 1)
                attention0(half, 1)
                layer_norm(half, 2)
                mlp_block(half, 0)
                layer_norm(half, 3)
                pe.wait_ge(S.qz_ready, (half + 1) * 2)
                attention1(half)
                layer_norm(half, 4)
                mlp_block(half, 1)
                x_out(half)

        @block.scalar
        def _(act):
            def high(dst, src, bias=0.0):
                return nc.scalar.activation(dst, src, ACT.Identity, bias=bias)

            def split_context(i):
                for b in range(2):
                    o = b * (U.shape[2] // 2)
                    act.wait_ge(S.raw_in[b], i * (16 * TC) + 16 * TC)
                    act.wait_ge(S.c_out[b], START + i * 32)
                    high(by_chunk(U[:, 0, o:o + NAT]), raw_ctx[:, b].rearrange("p t (c k) -> p t c k", c=DC))\
                        .then_inc(S.c_hi[b], 1)
                    for c in range(DC):
                        act.wait_ge(S.c_mm, i * (2 * DC) + b * DC + c + 1)
                        a = o + NAT + c * LT
                        high(U[:, 0, a:a + LT], bank[b * DC + c][:, 0:LT]).then_inc(S.c_hi[b], 1)
                    act.wait_ge(S.c_hi[b], START + i * (1 + DC) + 1 + DC)
                    act.wait_ge(S.c_lo[b], START + i * (1 + DC) + 1 + DC)
                    for p_ in range(2):
                        act.dma_start(ctx_dram[bass.ds(i * 2 + b, 1), :, p_].rearrange("o p n -> p (o n)"),
                                      f32(U[:, p_, o:o + NAT + TRA])).then_inc(S.c_out[b], 16)

            with act.Fori(0, BATCH // 2) as i:
                split_context(i)

            def layer_norm(half, l):
                li = half * NORMS + l
                offset, then = norms[l][1], norms[l][3]
                nc.scalar.activation(table_load[:, 0:1], eps, ACT.Sqrt)
                for c in range(DC):
                    act.wait_ge(S.ln_cent, li * DC + c + 1)
                    if c >= 2:
                        act.wait_ge(S.ln_var, li * DC + c - 1)
                    nc.scalar.activation(tmp[:, c % 2, :], centred[:, c, :], ACT.Square).then_inc(S.ln_sq, 1)
                act.wait_ge(S.ln_var, (li + 1) * DC)
                nc.scalar.activation(tmp[:, 0, :], bank[1][:, 0:ROWS], ACT.Sqrt, bias=eps).then_inc(S.ln_std, 1)
                nc.scalar.activation(table_load[:, 1:2], eps, then)
                for c in range(DC):
                    act.wait_ge(S.ln_y, li * DC + c + 1)
                    high(hT_c(0, c), centred[:, c, :], cols[:, col[offset] + c:col[offset] + c + 1])\
                        .then_inc(S.ln_hi, 1)

            def attention0(half, layer):
                with act.Fori(0, GROUPS) as g:
                    it, n = att0_step(half, layer, g)
                    B = it * UNITS

                    def head_col(name, h):
                        return cols[:, bass.ds(g * HG + (col[f"L0_xattn_{name}{layer + 1}"] + h), 1)]

                    for h in range(HG):
                        reached = act.to_reg(done(n, T0["q", h]))
                        act.wait_ge(S.cols_ready, 1)
                        act.wait_ge(S.w_done, reached)
                        high(qT[:, 0, h * ROWS:(h + 1) * ROWS], bank[h % 2][:, 0:ROWS], head_col("bq", h))\
                            .then_inc(S.q_hi, 1)

                    def keys(u):
                        b, h = divmod(u, HG)
                        if b == NB - 1:
                            reached = act.to_reg(done(n, T0["k", h]))
                            act.wait_ge(S.cols_ready, 1)
                            act.wait_ge(S.w_done, reached)
                        else:
                            reached = act.to_reg(START + it * ((NB - 1) * HG) + u + 1)
                            act.wait_ge(S.cols_ready, 1)
                            act.wait_ge(S.k_mm, reached)
                        high(kT[:, u % 2, 0, 1:LT], bank[u % 2][:, 1:LT], head_col("bk", h)).then_inc(S.k_hi, 1)

                    def p_turned(u):
                        b, h = divmod(u, HG)
                        act.wait_ge(S.t_mm, START + B + u + 1)
                        if h == 0:
                            act.wait_ge(S.p0_ready, START + it * NB + max(b - 1, 0))
                        dst = pT[:, b % 2, 0, :].rearrange("p (t n) -> p t n", t=TC)[:, :, h * LQ:(h + 1) * LQ]
                        high(dst, bank[4 + u % 2][:, 0:TC * LQ].rearrange("p (t n) -> p t n", t=TC))\
                            .then_inc(S.pt_hi, 1)

                    def exponent(u):
                        act.wait_ge(S.nm_ready, B + u + 1)
                        x = prob[0:LQ, u % PB, 0:LT]
                        nc.scalar.activation(x, x, ACT.Exp, scale=-1.0, bias=nmax[0:LQ, u % PB:u % PB + 1],
                                             accum_out=denom[0:LQ, u % PB:u % PB + 1]).then_inc(S.exp_ready, 1)

                    def applied(b, c):
                        act.wait_ge(S.u_mm, START + it * (NB * DC) + b * DC + c + 1)
                        dst = U[:, 0, c * HG * ROWS:(c + 1) * HG * ROWS]\
                            .rearrange("p (h n) -> p h n", h=HG)[:, :, b * LQ:(b + 1) * LQ]
                        high(dst, bank[6 + c % 2][:, 0:ROWS].rearrange("p (h n) -> p h n", h=HG))\
                            .then_inc(S.u_hi, 1)

                    for s in STEPS0:
                        if s < UNITS:
                            keys(s)
                        if s >= LAG:
                            p_turned(s - LAG)
                        if 1 <= s < UNITS:
                            exponent(s - 1)
                        for b, c in APPLY.get(s, []):
                            applied(b, c)
                        if s == UNITS:
                            exponent(s - 1)
                    for h in range(HG):
                        reached = act.to_reg(START + it * HG + h + 1)
                        act.wait_ge(S.cols_ready, 1)
                        act.wait_ge(S.v_tmp, reached)
                        if h >= 2:
                            act.wait_ge(S.w_done, done(n, T0["o", h - 2]))
                        high(part[:, h % 2, 0, :], tmp[:, h % 2, :], head_col("bv", h)).then_inc(S.v_hi, 1)

            def mlp_block(half, m):
                bias, gelu = mlp[m][2:]
                with act.Fori(0, MLP_STEPS) as st:
                    M, n = mlp_step(half, m, st)
                    for f in range(MLP_F):
                        reached = act.to_reg(done(n, TM["a", f]))
                        act.wait_ge(S.cols_ready, 1)
                        act.wait_ge(S.w_done, reached)
                        if f >= 2:
                            reached = act.to_reg(M * MLP_F + f - 1)
                            act.wait_ge(S.cols_ready, 1)
                            act.wait_ge(S.m_lo, reached)
                        nc.scalar.activation(tmp[:, f % 2, :], bank[f % 2][:, 0:ROWS], gelu,
                                             bias=cols[:, bass.ds(st * MLP_F + (col[bias] + f), 1)])\
                            .then_inc(S.m_gelu, 1)
                        act.wait_ge(S.m_gelu, START + M * MLP_F + f + 1)
                        high(part[:, f % 2, 0, :], tmp[:, f % 2, :]).then_inc(S.m_hi, 1)

            def attention1(half):
                n = half * HALF_TILES + ATT1_BASE
                act.wait_ge(S.qz_ready, (half + 1) * 2)
                for j in range(4):
                    act.wait_ge(S.w_done, done(n, T1["q", j]))
                    for i in range(HG):
                        r, a = slice(i * HD1, (i + 1) * HD1), (j * HG + i) * ROWS
                        high(q_masked[r, 0, a:a + ROWS], bank[j % 2][r, 0:ROWS],
                             cols[r, col["L1_xattn_q_b"] + j:col["L1_xattn_q_b"] + j + 1]).then_inc(S.q1_hi, 1)

                def values(b):
                    for t in range(TC):
                        if b == NB - 1 and t == TC - 1:
                            act.wait_ge(S.w_done, done(n, T1["v", 3]))
                        else:
                            act.wait_ge(S.v1_mm, half * (NB * TC - 1) + b * TC + t + 1)
                        high(v1[b % 2][0:TK[t], 0, t * D:(t + 1) * D], bank[V1_BANK[t]][0:TK[t], :])\
                            .then_inc(S.v1_hi, 1)

                def keys(s):
                    b, j = divmod(s, 4)
                    if b == NB - 1:
                        act.wait_ge(S.w_done, done(n, T1["k", j]))
                    else:
                        act.wait_ge(S.k1_mm, half * ((NB - 1) * 4) + s + 1)
                    high(kT[:, s % 2, 0, :], bank[s % 2][:, 0:LT],
                         cols[:, col["L1_xattn_k_b"] + j:col["L1_xattn_k_b"] + j + 1]).then_inc(S.k1_hi, 1)

                def p_turned(u):
                    s, i = divmod(u, HG)
                    act.wait_ge(S.t1_mm, START + half * U1 + u + 1)
                    dst = pT[:, s % 2, 0, :].rearrange("p (t n) -> p t n", t=TC)[:, :, i * LQ:(i + 1) * LQ]
                    high(dst, bank[4 + u % 2][:, 0:TC * LQ].rearrange("p (t n) -> p t n", t=TC))\
                        .then_inc(S.pt1_hi, 1)

                def exponent(u):
                    act.wait_ge(S.nm1_ready, START + half * U1 + u + 1)
                    x = prob[0:LQ, u % PB, 1:LT]
                    nc.scalar.activation(x, x, ACT.Exp, scale=-1.0, bias=nmax[0:LQ, u % PB:u % PB + 1],
                                         accum_out=denom[0:LQ, u % PB:u % PB + 1]).then_inc(S.exp1_ready, 1)

                def normalise(u):
                    act.wait_ge(S.rden1_ready, half * U1 + u + 1)
                    x = prob[0:LQ, u % PB, 1:LT]
                    nc.scalar.activation(x, x, ACT.Identity, scale=rden[0:LQ, u % PB:u % PB + 1]).then_inc(S.p1_act, 1)

                def applied(s):
                    b, j = divmod(s, 4)
                    act.wait_ge(S.a_mm, half * G1 + s + 1)
                    for i in range(HG):
                        r, a = slice(i * HD1, (i + 1) * HD1), j * ROWS + b * LQ
                        high(attnT[r, 0, a:a + LQ], bank[6 + s % 2][r, i * LQ:(i + 1) * LQ],
                             cols[r, col["L1_xattn_v_b"] + j:col["L1_xattn_v_b"] + j + 1]).then_inc(S.a_hi, 1)

                for s in range(G1 + 3):
                    if s < G1 and s % 4 == 0:
                        values(s // 4)
                    for i in range(HG):
                        u = (s - 1) * HG + i
                        if s < G1 and i == HG - 2:
                            keys(s)
                        if 0 <= u - LAG < U1:
                            p_turned(u - LAG)
                        if 0 <= u < U1:
                            exponent(u)
                        if 0 <= u - 1 < U1 and by_act(u - 1):
                            normalise(u - 1)
                    if s >= 3:
                        applied(s - 3)

            with act.Fori(0, 2) as half:
                layer_norm(half, 0)
                attention0(half, 0)
                layer_norm(half, 1)
                attention0(half, 1)
                layer_norm(half, 2)
                mlp_block(half, 0)
                layer_norm(half, 3)
                attention1(half)
                layer_norm(half, 4)
                mlp_block(half, 1)
                for b in range(NB):
                    reached = act.to_reg(START + half * NB + b + 1)
                    act.wait_ge(S.cols_ready, 1)
                    act.wait_ge(S.out_copied, reached)
                    act.dma_start(out[bass.ds(half * NB + b, 1)].rearrange("o q d -> (o q) d"),
                                  out_nat[0:LQ, b % 2, :]).then_inc(S.out_saved[b % 2], 16)

        @block.vector
        def _(dve):
            def low(dst, src, bias, hi):
                return nc.vector.scalar_tensor_tensor(out=dst, in0=src, scalar=bias, in1=f32(hi),
                                                      op0=ALU.add, op1=ALU.subtract)

            def rest(dst, src, hi):
                return nc.vector.tensor_tensor(dst, src, f32(hi), ALU.subtract)

            nc.vector.memset(raw_inputs[:, 0:2 * NAT], 0.0).then_inc(S.raw_cleared, 1)
            nc.vector.memset(eps, EPS).then_inc(S.extra_a, 1)
            nc.vector.memset(mean_w[:], 1.0 / D).then_inc(S.mean_ready, 1)

            def split_context(i):
                for b in range(2):
                    o = b * (U.shape[2] // 2)
                    dve.wait_ge(S.c_hi[b], START + i * (1 + DC) + 1)
                    rest(by_chunk(U[:, 1, o:o + NAT]), raw_ctx[:, b].rearrange("p t (c k) -> p t c k", c=DC),
                         by_chunk(U[:, 0, o:o + NAT])).then_inc(S.c_lo[b], 1)
                    for c in range(DC):
                        dve.wait_ge(S.c_hi[b], START + i * (1 + DC) + c + 2)
                        a = o + NAT + c * LT
                        rest(U[:, 1, a:a + LT], bank[b * DC + c][:, 0:LT], U[:, 0, a:a + LT]).then_inc(S.c_lo[b], 1)

            with dve.Fori(0, BATCH // 2) as i:
                split_context(i)
            dve.wait_ge(S.cols_mm, ncol_tiles)
            nc.vector.tensor_copy(cols[:], bank[0][:, 0:ncol_tiles * P]).then_inc(S.cols_ready, 1)
            nc.vector.memset(prob[:], 0.0).then_inc(S.prob_cleared, 1)
            dve.wait_ge(S.cols_ready, 1)
            for layer in range(2):
                bk = col[f"L0_xattn_bias_k{layer + 1}"]
                bias_v, bv = col[f"L0_xattn_bias_v{layer + 1}"], col[f"L0_xattn_bv{layer + 1}"]
                nc.vector.tensor_copy(extra_k[:, layer, :, 0], cols[:, bk:bk + HEADS0]).then_inc(S.extra_a, 1)
                dve.wait_ge(S.extra_a, 2 + layer)
                nc.vector.tensor_tensor(extra_k[:, layer, :, 1], cols[:, bk:bk + HEADS0],
                                        f32(extra_k[:, layer, :, 0]), ALU.subtract).then_inc(S.extra_ready, 1)
                nc.vector.tensor_tensor(extra_v[:, layer, :], cols[:, bias_v:bias_v + HEADS0],
                                        cols[:, bv:bv + HEADS0], ALU.subtract).then_inc(S.extra_ready, 1)
            dve.wait_ge(S.extra_ready, 4)
            dve.wait_ge(S.prob_cleared, 1)

            def x_in(half):
                for b in range(NB):
                    dve.wait_ge(S.x_mm, START + half * NB + b + 1)
                    nc.vector.tensor_copy(xT[:, :, b * LQ:(b + 1) * LQ],
                                          bank[4 + b][:, 0:DC * LQ].rearrange("p (c n) -> p c n", c=DC))\
                        .then_inc(S.x_ready, 1)
                for b in range(2):
                    dve.wait_ge(S.out_saved[b], START + half * 32)

            def x_out(half):
                for b in range(NB):
                    dve.wait_ge(S.out_mm, half * NB + b + 1)
                    if b >= 2:
                        dve.wait_ge(S.out_saved[b % 2], START + half * 32 + 16)
                    nc.vector.tensor_copy(out_nat[0:LQ, b % 2, :], bank[6 + b % 2][0:LQ, :]).then_inc(S.out_copied, 1)

            def add_to_x(added, chunk_mm, chunks, last_tile):
                for c in range(DC):
                    if c < DC - 1:
                        dve.wait_ge(chunk_mm, chunks * (DC - 1) + c + 1)
                    else:
                        dve.wait_ge(S.w_done, last_tile)
                    nc.vector.tensor_tensor(xT[:, c, :], xT[:, c, :], bank[2 + c][:, 0:ROWS], ALU.add)\
                        .then_inc(added, 1)

            def layer_norm(half, l):
                li = half * NORMS + l
                scale, offset, bias = norms[l][:3]
                dve.wait_ge(S.ln_mm, li + 1)
                for c in range(DC):
                    nc.vector.tensor_tensor(centred[:, c, :], xT[:, c, :], bank[0][:, 0:ROWS], ALU.subtract)\
                        .then_inc(S.ln_cent, 1)
                for c in range(DC):
                    nc.vector.tensor_scalar(xT[:, c, :], xT[:, c, :], cols[:, col[bias] + c:col[bias] + c + 1], None,
                                            ALU.add).then_inc(S.ln_bias, 1)
                dve.wait_ge(S.ln_std, li + 1)
                nc.vector.reciprocal(tmp[:, 1, :], tmp[:, 0, :]).then_inc(S.ln_rstd, 1)

                def scaled(c):
                    nc.vector.scalar_tensor_tensor(
                        out=centred[:, c, :], in0=centred[:, c, :], scalar=cols[:, col[scale] + c:col[scale] + c + 1],
                        in1=tmp[:, 1, :], op0=ALU.mult, op1=ALU.mult).then_inc(S.ln_y, 1)

                def split(c):
                    dve.wait_ge(S.ln_hi, li * DC + c + 1)
                    low(hT_c(1, c), centred[:, c, :], cols[:, col[offset] + c:col[offset] + c + 1], hT_c(0, c))\
                        .then_inc(S.ln_lo, 1)

                dve.wait_ge(S.ln_rstd, li + 1)
                dve.wait_ge(S.ln_cent, (li + 1) * DC)
                scaled(0)
                for c in range(1, DC):
                    scaled(c)
                    split(c - 1)
                split(DC - 1)
                reached = dve.to_reg((li + 1) * DC)
                dve.wait_ge(S.cols_ready, 1)
                dve.wait_ge(S.ln_bias, reached)

            def attention0(half, layer):
                with dve.Fori(0, GROUPS) as g:
                    it, n = att0_step(half, layer, g)
                    B = it * UNITS

                    def head_col(name, h):
                        return cols[:, bass.ds(g * HG + (col[f"L0_xattn_{name}{layer + 1}"] + h), 1)]

                    for h in range(HG):
                        dve.wait_ge(S.q_hi, it * HG + h + 1)
                        low(qT[:, 1, h * ROWS:(h + 1) * ROWS], bank[h % 2][:, 0:ROWS], head_col("bq", h),
                            qT[:, 0, h * ROWS:(h + 1) * ROWS]).then_inc(S.q_lo, 1)

                    def keys(u):
                        b, h = divmod(u, HG)
                        dve.wait_ge(S.k_hi, B + u + 1)
                        nc.vector.tensor_scalar(kT[:, u % 2, :, 0],
                                                f32(extra_k[:, layer, bass.ds(g * HG + h, 1), :])
                                                .rearrange("p o n -> p (o n)"), 1.0, None, ALU.mult)\
                            .then_inc(S.k_col, 1)
                        low(kT[:, u % 2, 1, 1:LT], bank[u % 2][:, 1:LT], head_col("bk", h), kT[:, u % 2, 0, 1:LT])\
                            .then_inc(S.k_lo, 1)

                    def maximum(u):
                        dve.wait_ge(S.s_mm, B + u + 1)
                        dve.wait_ge(S.t_mm, START + B + max(u - PB + 1, 0))
                        nc.vector.tensor_scalar(prob[0:LQ, u % PB, 0:LT], bank[2 + u % 2][0:LQ, 0:LT], -SCALE0, None,
                                                ALU.mult, ALU.min, accum_out=nmax[0:LQ, u % PB:u % PB + 1])\
                            .then_inc(S.nm_ready, 1)

                    def normalise(u):
                        dve.wait_ge(S.exp_ready, B + u + 1)
                        d, r = denom[0:LQ, u % PB:u % PB + 1], rden[0:LQ, u % PB:u % PB + 1]
                        nc.vector.reciprocal(r, d).then_inc(S.rden_ready, 1)
                        dve.wait_ge(S.rden_ready, B + u + 1)
                        x = prob[0:LQ, u % PB, 0:LT]
                        nc.vector.tensor_scalar(x, x, r, None, ALU.mult).then_inc(S.p_ready, 1)

                    def p_turned(u):
                        b, h = divmod(u, HG)
                        dve.wait_ge(S.pt_hi, B + u + 1)
                        hi, lo = (pT[:, b % 2, p_, :].rearrange("p (t n) -> p t n", t=TC)[:, :, h * LQ:(h + 1) * LQ]
                                  for p_ in range(2))
                        rest(lo, bank[4 + u % 2][:, 0:TC * LQ].rearrange("p (t n) -> p t n", t=TC), hi)\
                            .then_inc(S.pt_lo, 1)

                    def applied(b, c):
                        dve.wait_ge(S.u_hi, it * (NB * DC) + b * DC + c + 1)
                        hi, lo = (U[:, p_, c * HG * ROWS:(c + 1) * HG * ROWS]
                                  .rearrange("p (h n) -> p h n", h=HG)[:, :, b * LQ:(b + 1) * LQ]
                                  for p_ in range(2))
                        rest(lo, bank[6 + c % 2][:, 0:ROWS].rearrange("p (h n) -> p h n", h=HG), hi)\
                            .then_inc(S.u_lo, 1)

                    for s in STEPS0:
                        if s < UNITS:
                            keys(s)
                        if 1 <= s < UNITS:
                            maximum(s - 1)
                        if s >= LAG:
                            p_turned(s - LAG)
                        if 1 <= s < UNITS:
                            normalise(s - 1)
                        for b, c in APPLY.get(s, []):
                            applied(b, c)
                        if s == UNITS:
                            maximum(s - 1)
                            normalise(s - 1)

                    def value_sum(h):
                        dve.wait_ge(S.w_done, done(n, T0["v", h]))
                        if h == 0:
                            dve.wait_ge(S.p0_ready, START + (it + 1) * NB)
                        if h >= 2:
                            dve.wait_ge(S.v_lo, it * HG + h - 1)
                        nc.vector.scalar_tensor_tensor(
                            out=tmp[:, h % 2, :].rearrange("p (b n) -> p b n", b=NB),
                            in0=p0_all[:, :, h * LQ:(h + 1) * LQ],
                            scalar=extra_v[:, layer, bass.ds(g * HG + h, 1)],
                            in1=bank[6 + h % 2][:, 0:ROWS].rearrange("p (b n) -> p b n", b=NB),
                            op0=ALU.mult, op1=ALU.add).then_inc(S.v_tmp, 1)

                    def value_low(h):
                        dve.wait_ge(S.v_hi, it * HG + h + 1)
                        low(part[:, h % 2, 1, :], tmp[:, h % 2, :], head_col("bv", h), part[:, h % 2, 0, :])\
                            .then_inc(S.v_lo, 1)

                    value_sum(0)
                    for h in range(1, HG):
                        value_low(h - 1)
                        value_sum(h)
                    value_low(HG - 1)
                    add_to_x(S.x_add, S.o_mm, it, done(n, T0["o", HG - 1]))

            def mlp_block(half, m):
                with dve.Fori(0, MLP_STEPS) as st:
                    M, n = mlp_step(half, m, st)
                    for f in range(MLP_F):
                        dve.wait_ge(S.m_hi, M * MLP_F + f + 1)
                        rest(part[:, f % 2, 1, :], tmp[:, f % 2, :], part[:, f % 2, 0, :]).then_inc(S.m_lo, 1)
                    add_to_x(S.m_add, S.m_mm, M, done(n, TM["b", MLP_F - 1]))

            def attention1(half):
                n = half * HALF_TILES + ATT1_BASE
                nc.vector.memset(prob[0:LQ, :, 0:1], 0.0).then_inc(S.p1_cleared, 1)
                dve.wait_ge(S.p1_cleared, half + 1)
                for j in range(4):
                    for i in range(HG):
                        r, a = slice(i * HD1, (i + 1) * HD1), (j * HG + i) * ROWS
                        dve.wait_ge(S.q1_hi, half * 16 + j * HG + i + 1)
                        low(q_masked[r, 1, a:a + ROWS], bank[j % 2][r, 0:ROWS],
                            cols[r, col["L1_xattn_q_b"] + j:col["L1_xattn_q_b"] + j + 1],
                            q_masked[r, 0, a:a + ROWS]).then_inc(S.q1_lo, 1)

                def values(b):
                    for t in range(TC):
                        dve.wait_ge(S.v1_hi, half * (NB * TC) + b * TC + t + 1)
                        hi, lo = (v1[b % 2][0:TK[t], p_, t * D:(t + 1) * D] for p_ in range(2))
                        rest(lo, bank[V1_BANK[t]][0:TK[t], :], hi).then_inc(S.v1_lo, 1)

                def keys(s):
                    b, j = divmod(s, 4)
                    dve.wait_ge(S.k1_hi, half * G1 + s + 1)
                    low(kT[:, s % 2, 1, :], bank[s % 2][:, 0:LT],
                        cols[:, col["L1_xattn_k_b"] + j:col["L1_xattn_k_b"] + j + 1], kT[:, s % 2, 0, :])\
                        .then_inc(S.k1_lo, 1)

                def maximum(u):
                    b = u // HEADS0
                    reached = dve.to_reg(half * U1 + u + 1)
                    dve.wait_ge(S.cols_ready, 1)
                    dve.wait_ge(S.s1_mm, reached)
                    dve.wait_ge(S.t1_mm, START + half * U1 + max(u - PB + 1, 0))
                    if u % HEADS0 == 0:
                        dve.wait_ge(S.mask_ready, START + half * NB + b + 1)
                    nc.vector.tensor_tensor_reduce(out=prob[0:LQ, u % PB, 1:LT], in0=bank[2 + u % 2][0:LQ, 1:LT],
                                                   in1=mask_off[0:LQ, b % 2, 1:LT], scale=-SCALE1, scalar=FMAX,
                                                   op0=ALU.add, op1=ALU.min, accum_out=nmax[0:LQ, u % PB:u % PB + 1])\
                        .then_inc(S.nm1_ready, 1)

                def inverse(u):
                    dve.wait_ge(S.exp1_ready, half * U1 + u + 1)
                    nc.vector.reciprocal(rden[0:LQ, u % PB:u % PB + 1], denom[0:LQ, u % PB:u % PB + 1])\
                        .then_inc(S.rden1_ready, 1)

                def normalise(u):
                    dve.wait_ge(S.rden1_ready, half * U1 + u + 1)
                    x = prob[0:LQ, u % PB, 1:LT]
                    nc.vector.tensor_scalar(x, x, rden[0:LQ, u % PB:u % PB + 1], None, ALU.mult)\
                        .then_inc(S.p1_ready, 1)

                def p_turned(u):
                    s, i = divmod(u, HG)
                    dve.wait_ge(S.pt1_hi, half * U1 + u + 1)
                    hi, lo = (pT[:, s % 2, p_, :].rearrange("p (t n) -> p t n", t=TC)[:, :, i * LQ:(i + 1) * LQ]
                              for p_ in range(2))
                    rest(lo, bank[4 + u % 2][:, 0:TC * LQ].rearrange("p (t n) -> p t n", t=TC), hi)\
                        .then_inc(S.pt1_lo, 1)

                def applied(s):
                    b, j = divmod(s, 4)
                    for i in range(HG):
                        r, a = slice(i * HD1, (i + 1) * HD1), j * ROWS + b * LQ
                        dve.wait_ge(S.a_hi, half * (G1 * HG) + s * HG + i + 1)
                        low(attnT[r, 1, a:a + LQ], bank[6 + s % 2][r, i * LQ:(i + 1) * LQ],
                            cols[r, col["L1_xattn_v_b"] + j:col["L1_xattn_v_b"] + j + 1], attnT[r, 0, a:a + LQ])\
                            .then_inc(S.a_lo, 1)

                for s in range(G1 + 3):
                    if s < G1 and s % 4 == 0:
                        values(s // 4)
                    for i in range(HG):
                        u = (s - 1) * HG + i
                        if 0 <= u < U1:
                            maximum(u)
                        if s < G1 and i == HG - 2:
                            keys(s)
                        if 0 <= u - 1 < U1:
                            inverse(u - 1)
                        if 0 <= u - LAG < U1:
                            p_turned(u - LAG)
                        if 0 <= u - 1 < U1 and not by_act(u - 1):
                            normalise(u - 1)
                    if s >= 3:
                        applied(s - 3)
                add_to_x(S.c_add, S.cproj_mm, half, done(n, T1["c", 3]))

            with dve.Fori(0, 2) as half:
                x_in(half)
                layer_norm(half, 0)
                attention0(half, 0)
                layer_norm(half, 1)
                attention0(half, 1)
                layer_norm(half, 2)
                mlp_block(half, 0)
                layer_norm(half, 3)
                attention1(half)
                layer_norm(half, 4)
                mlp_block(half, 1)
                x_out(half)


_LAYER0 = [f"L0_xattn_{x}{n}" for n in (1, 2) for x in
           ("wq", "bq", "wk", "bk", "wv", "bv", "wo", "bo", "bias_k", "bias_v")]
_INS = ["x", "ctx_2048", "mask_BxS2_bf1", *_LAYER0,
        "L0_xattn_ln1_scale", "L0_xattn_ln1_offset", "L0_xattn_ln2_scale", "L0_xattn_ln2_offset",
        "L0_xattn_ln_mlp_scale", "L0_xattn_ln_mlp_offset",
        "L0_xattn_w_fc1", "L0_xattn_b_fc1", "L0_xattn_w_fc2", "L0_xattn_b_fc2",
        "L1_xattn_ln1_w", "L1_xattn_ln1_b", "L1_xattn_q_w", "L1_xattn_q_b", "L1_xattn_k_w", "L1_xattn_k_b",
        "L1_xattn_v_w", "L1_xattn_v_b", "L1_xattn_cproj_w", "L1_xattn_cproj_b", "L1_xattn_ln2_w",
        "L1_xattn_ln2_b", "L1_xattn_fc_w", "L1_xattn_fc_b", "L1_xattn_proj_w", "L1_xattn_proj_b"]


def kernel(**inputs):
    import numpy as _np
    import concourse.bacc as _bacc
    from concourse import mybir as _mybir
    from concourse.bass_utils import run_bass_kernel_spmd as _run

    nc = _bacc.Bacc("TRN2", target_bir_lowering=False, num_devices=1)
    arrays, tensors = {}, {}
    for name in _INS:
        a = _np.ascontiguousarray(inputs[name])
        if a.dtype.kind == "b":
            a = a.view(_np.uint8)
        arrays[f"in_{name}"] = a
        tensors[name] = nc.dram_tensor(f"in_{name}", a.shape, _mybir.dt.from_np(a.dtype), kind="ExternalInput").ap()
    out = nc.dram_tensor("out_0", (BATCH, LQ, D), F32, kind="ExternalOutput").ap()
    build(nc, tensors, out)
    r = _run(nc, [arrays], core_ids=[0])
    return r.results[0]["out_0"]
```
